# Optimizing a Trainium2 kernel written in Bass

```python
import numpy as np
import jax
import jax.numpy as jnp

def _softmax(x, axis=-1):
    return jax.nn.softmax(x, axis=axis)

def _gelu(x):
    return jax.nn.gelu(x, approximate=True)

def _silu(x):
    return jax.nn.silu(x)

def _sigmoid(x):
    return jax.nn.sigmoid(x)

def _layernorm(x, axis=-1, eps=1e-05):
    m = jnp.mean(x, axis=axis, keepdims=True)
    v = jnp.var(x, axis=axis, keepdims=True)
    return (x - m) / jnp.sqrt(v + eps)

def _scatter_add(tgt, idx, src, axis=0):
    return tgt.at[idx].add(src)

def _segment_sum(src, seg, n):
    return jax.ops.segment_sum(src, seg, n)
kernel_name = 'mk_xattn_ffn_d4_seqx_r4_a3c9ac'

def setup_inputs(seed: int=0):
    np.random.seed(seed)
    _w = jnp.asarray

    def _rec_inputs():
        import jax
        import jax.numpy as jnp
        _rk = jax.random.key(seed)
        x = 7.22e-05 + 1 * jax.random.normal(jax.random.fold_in(_rk, 1), (1, 2048, 256), jnp.float32)
        _lenS = 2048 - jax.random.randint(jax.random.fold_in(_rk, 7), (1,), 0, max(1, 2048 // 4) + 1, jnp.int32)
        _lenS2 = 1601 - jax.random.randint(jax.random.fold_in(_rk, 8), (1,), 0, max(1, 1601 // 4) + 1, jnp.int32)
        _ctx_768P = jax.random.normal(jax.random.fold_in(_rk, 11), (1, 16, 192), jnp.float32)
        _ctx_768c = jax.random.dirichlet(jax.random.fold_in(_rk, 511), 0.3 * jnp.ones((16,), jnp.float32), (1, 1601))
        _ctx_768t = jnp.einsum('bsk,bkd->bsd', _ctx_768c, _ctx_768P)
        _ctx_768t = _ctx_768t * jax.lax.rsqrt(jnp.mean(jnp.square(_ctx_768t)) + 1e-12) * 0.953939
        ctx_768 = -0.000191848 + 0.999787 * (_ctx_768t + 0.3 * jax.random.normal(jax.random.fold_in(_rk, 611), (1, 1601, 192), jnp.float32))
        _validS = jnp.arange(2048)[None, :] < _lenS[:, None]
        _validS2 = jnp.arange(1601)[None, :] < _lenS2[:, None]
        _causal = jnp.tril(jnp.ones((2048, 2048), dtype=bool))
        mask_BxS2_bf1 = jnp.ones((1, 1601), dtype=bool)
        return (x, ctx_768, mask_BxS2_bf1)
    x, ctx_768, mask_BxS2_bf1 = _rec_inputs()

    def _L0_xattn_setup():
        import jax, jax.numpy as jnp
        import numpy as np
        N_HEADS = 16
        key = jax.random.key(seed)
        ks = jax.random.split(key, 8)
        b, l, m = (8, 256, 256)
        d_embed, d_cross = (256, 192)
        s_q = 1.0 / np.sqrt(d_embed)
        s_kv = 1.0 / np.sqrt(d_cross)
        return {'x': jax.random.normal(ks[0], (b, l, d_embed), jnp.float32), 'y': jax.random.normal(ks[1], (b, m, d_cross), jnp.float32), 'Wq': jax.random.normal(ks[2], (d_embed, d_embed), jnp.float32) * s_q, 'bq': jax.random.normal(ks[3], (d_embed,), jnp.float32) * 0.01, 'Wkv': jax.random.normal(ks[4], (2 * d_embed, d_cross), jnp.float32) * s_kv, 'bkv': jax.random.normal(ks[5], (2 * d_embed,), jnp.float32) * 0.01, 'Wo': jax.random.normal(ks[6], (d_embed, d_embed), jnp.float32) * s_q, 'bo': jax.random.normal(ks[7], (d_embed,), jnp.float32) * 0.01}
    _L0_xattn_all = _L0_xattn_setup()
    _L0_xattn_in = {k: v for k, v in _L0_xattn_all.items() if k in ('Wq', 'bq', 'Wkv', 'bkv', 'Wo', 'bo')}
    del _L0_xattn_all

    def _L0_ffn_setup():
        import jax, jax.numpy as jnp
        import numpy as np
        TOP_K = 4
        N_GROUP = 4
        TOPK_GROUP = 2
        ROUTED_SCALING = 2.5

        def _route(x, gate_weight):
            scores = jax.nn.sigmoid(x @ gate_weight.T)
            T, E = scores.shape
            gs = E // N_GROUP
            top2, _ = jax.lax.top_k(scores.reshape(T, N_GROUP, gs), 2)
            group_scores = top2.sum(-1)
            _, gidx = jax.lax.top_k(group_scores, TOPK_GROUP)
            gmask = jax.nn.one_hot(gidx, N_GROUP, dtype=jnp.float32).sum(1)
            smask = jnp.repeat(gmask, gs, axis=1) > 0.5
            masked = jnp.where(smask, scores, 0.0)
            topk_idx = jax.lax.top_k(masked, TOP_K)[1]
            topk_w = jnp.take_along_axis(scores, topk_idx, axis=1)
            topk_w = topk_w / (topk_w.sum(-1, keepdims=True) + 1e-20)
            topk_w = topk_w * ROUTED_SCALING
            combine = jnp.zeros((T, E), jnp.float32).at[jnp.arange(T)[:, None], topk_idx].add(topk_w)
            return combine
        key = jax.random.key(seed)
        ks = jax.random.split(key, 6)
        B, S, H = (2, 256, 256)
        E, I, Is = (16, 128, 512)
        g = lambda k, shape, scale: jax.random.normal(k, shape, dtype=jnp.float32) * scale
        return {'hidden_states': g(ks[0], (B, S, H), 1.0), 'gate_weight': g(ks[1], (E, H), 0.02), 'expert_up': g(ks[2], (E, H, I), 0.02), 'expert_down': g(ks[3], (E, I, H), 0.02), 'shared_up': g(ks[4], (H, Is), 0.02), 'shared_down': g(ks[5], (Is, H), 0.02)}
    _L0_ffn_all = _L0_ffn_setup()
    _L0_ffn_in = {k: v for k, v in _L0_ffn_all.items() if k in ('gate_weight', 'expert_up', 'expert_down', 'shared_up', 'shared_down')}
    del _L0_ffn_all

    def _L1_xattn_setup():
        import jax, jax.numpy as jnp
        import numpy as np
        N_HEADS = 16
        DIM_EMBED = 256
        DIM_CROSS = 192
        DIM_HEAD = DIM_EMBED // N_HEADS
        key = jax.random.key(seed)
        ks = jax.random.split(key, 10)
        B, Sq, Sk = (8, 1024, 77)
        s_e = 1.0 / np.sqrt(DIM_EMBED)
        s_c = 1.0 / np.sqrt(DIM_CROSS)
        return {'x': jax.random.normal(ks[0], (B, Sq, DIM_EMBED), jnp.float32), 'y': jax.random.normal(ks[1], (B, Sk, DIM_CROSS), jnp.float32), 'wq': jax.random.normal(ks[2], (DIM_EMBED, DIM_EMBED), jnp.float32) * s_e, 'bq': jax.random.normal(ks[3], (DIM_EMBED,), jnp.float32) * 0.01, 'wk': jax.random.normal(ks[4], (DIM_CROSS, DIM_EMBED), jnp.float32) * s_c, 'bk': jax.random.normal(ks[5], (DIM_EMBED,), jnp.float32) * 0.01, 'wv': jax.random.normal(ks[6], (DIM_CROSS, DIM_EMBED), jnp.float32) * s_c, 'bv': jax.random.normal(ks[7], (DIM_EMBED,), jnp.float32) * 0.01, 'wo': jax.random.normal(ks[8], (DIM_EMBED, DIM_EMBED), jnp.float32) * s_e, 'bo': jax.random.normal(ks[9], (DIM_EMBED,), jnp.float32) * 0.01}
    _L1_xattn_all = _L1_xattn_setup()
    _L1_xattn_in = {k: v for k, v in _L1_xattn_all.items() if k in ('wq', 'bq', 'wk', 'bk', 'wv', 'bv', 'wo', 'bo')}
    del _L1_xattn_all

    def _L1_ffn_setup():
        import jax, jax.numpy as jnp
        import numpy as np
        TOP_K = 2
        key = jax.random.key(seed)
        ks = jax.random.split(key, 6)
        B, T, H, E, F = (2, 512, 256, 8, 1024)
        s = 0.02
        return {'hidden_states': jax.random.normal(ks[0], (B, T, H), dtype=jnp.float32), 'router_w': jax.random.normal(ks[1], (E, H), dtype=jnp.float32) * s, 'w1': jax.random.normal(ks[2], (E, F, H), dtype=jnp.float32) * s, 'b1': jax.random.normal(ks[3], (E, F), dtype=jnp.float32) * s, 'w2': jax.random.normal(ks[4], (E, H, F), dtype=jnp.float32) * s, 'b2': jax.random.normal(ks[5], (E, H), dtype=jnp.float32) * s}
    _L1_ffn_all = _L1_ffn_setup()
    _L1_ffn_in = {k: v for k, v in _L1_ffn_all.items() if k in ('router_w', 'w1', 'b1', 'w2', 'b2')}
    del _L1_ffn_all

    def _L2_xattn_setup():
        import jax, jax.numpy as jnp
        import numpy as np
        import math
        N_HEADS = 8
        D_EMBED = 256
        D_CROSS = 192
        D_HEAD = D_EMBED // N_HEADS
        key = jax.random.key(seed)
        ks = jax.random.split(key, 10)
        B, S, SKV = (4, 768, 259)
        s_e = 1.0 / math.sqrt(D_EMBED)
        s_c = 1.0 / math.sqrt(D_CROSS)
        return {'x': jax.random.normal(ks[0], (B, S, D_EMBED), jnp.float32), 'y': jax.random.normal(ks[1], (B, SKV, D_CROSS), jnp.float32), 'Wq': jax.random.normal(ks[2], (D_EMBED, D_EMBED), jnp.float32) * s_e, 'bq': jnp.zeros((D_EMBED,), jnp.float32), 'Wk': jax.random.normal(ks[3], (D_EMBED, D_CROSS), jnp.float32) * s_c, 'bk': jnp.zeros((D_EMBED,), jnp.float32), 'Wv': jax.random.normal(ks[4], (D_EMBED, D_CROSS), jnp.float32) * s_c, 'bv': jnp.zeros((D_EMBED,), jnp.float32), 'Wo': jax.random.normal(ks[5], (D_EMBED, D_EMBED), jnp.float32) * s_e, 'bo': jnp.zeros((D_EMBED,), jnp.float32)}
    _L2_xattn_all = _L2_xattn_setup()
    _L2_xattn_in = {k: v for k, v in _L2_xattn_all.items() if k in ('Wq', 'bq', 'Wk', 'bk', 'Wv', 'bv', 'Wo', 'bo')}
    del _L2_xattn_all

    def _L2_ffn_setup():
        import jax, jax.numpy as jnp
        import numpy as np
        IN_DIM = 256
        OUT_DIM = 256
        NUM_EXPERTS = 8
        TOP_K = 2
        key = jax.random.key(seed)
        ks = jax.random.split(key, 5)
        s = 1.0 / np.sqrt(IN_DIM)
        x = jax.random.normal(ks[0], (4, 512, IN_DIM), dtype=jnp.float32)
        Wg = jax.random.uniform(ks[1], (IN_DIM, NUM_EXPERTS), jnp.float32, -s, s)
        bg = jnp.zeros((NUM_EXPERTS,), jnp.float32)
        We = jax.random.uniform(ks[2], (NUM_EXPERTS, OUT_DIM, IN_DIM), jnp.float32, -s, s)
        be = jax.random.uniform(ks[3], (NUM_EXPERTS, OUT_DIM), jnp.float32, -s, s)
        return {'x': x, 'Wg': Wg, 'bg': bg, 'We': We, 'be': be}
    _L2_ffn_all = _L2_ffn_setup()
    _L2_ffn_in = {k: v for k, v in _L2_ffn_all.items() if k in ('Wg', 'bg', 'We', 'be')}
    del _L2_ffn_all

    def _L3_xattn_setup():
        import jax, jax.numpy as jnp
        import numpy as np
        DIM = 256
        CTX_DIM = 192
        HEADS = 16
        key = jax.random.key(seed)
        ks = jax.random.split(key, 7)
        B, N, M = (4, 1024, 64)
        x = jax.random.normal(ks[0], (B, N, DIM), dtype=jnp.float32)
        context = jax.random.normal(ks[1], (B, M, CTX_DIM), dtype=jnp.float32)
        context_mask = jnp.ones((B, M), dtype=bool)
        s_d = 1.0 / np.sqrt(DIM)
        s_c = 1.0 / np.sqrt(CTX_DIM)
        Wq = jax.random.normal(ks[2], (DIM, DIM), dtype=jnp.float32) * s_d
        Wk = jax.random.normal(ks[3], (CTX_DIM, DIM), dtype=jnp.float32) * s_c
        Wv = jax.random.normal(ks[4], (CTX_DIM, DIM), dtype=jnp.float32) * s_c
        Wo = jax.random.normal(ks[5], (DIM, DIM), dtype=jnp.float32) * s_d
        return {'x': x, 'context': context, 'context_mask': context_mask, 'Wq': Wq, 'Wk': Wk, 'Wv': Wv, 'Wo': Wo}
    _L3_xattn_all = _L3_xattn_setup()
    _L3_xattn_in = {k: v for k, v in _L3_xattn_all.items() if k in ('Wq', 'Wk', 'Wv', 'Wo')}
    del _L3_xattn_all

    def _L3_ffn_setup():
        import jax, jax.numpy as jnp
        import numpy as np
        B, S, D = (1, 512, 256)
        F = 352
        E = 16
        K = 2
        CAP_FACTOR = 1.25

        def _mlp(h, wg, wu, wd):
            return jax.nn.silu(h @ wg) * (h @ wu) @ wd
        key = jax.random.key(seed)
        ks = jax.random.split(key, 10)
        sd = 0.02
        return {'x': jax.random.normal(ks[0], (B, S, D), jnp.float32), 'router_w': jax.random.normal(ks[1], (D, E), jnp.float32) * sd, 'router_b': jnp.zeros((E,), jnp.float32), 'w_gate': jax.random.normal(ks[2], (E, D, F), jnp.float32) * sd, 'w_up': jax.random.normal(ks[3], (E, D, F), jnp.float32) * sd, 'w_down': jax.random.normal(ks[4], (E, F, D), jnp.float32) * sd, 'sw_gate': jax.random.normal(ks[5], (D, F), jnp.float32) * sd, 'sw_up': jax.random.normal(ks[6], (D, F), jnp.float32) * sd, 'sw_down': jax.random.normal(ks[7], (F, D), jnp.float32) * sd}
    _L3_ffn_all = _L3_ffn_setup()
    _L3_ffn_in = {k: v for k, v in _L3_ffn_all.items() if k in ('router_w', 'router_b', 'w_gate', 'w_up', 'w_down', 'sw_gate', 'sw_up', 'sw_down')}
    del _L3_ffn_all
    return {'x': x, 'ctx_768': ctx_768, 'mask_BxS2_bf1': mask_BxS2_bf1, 'L0_xattn_Wq': _L0_xattn_in['Wq'], 'L0_xattn_bq': _L0_xattn_in['bq'], 'L0_xattn_Wkv': _L0_xattn_in['Wkv'], 'L0_xattn_bkv': _L0_xattn_in['bkv'], 'L0_xattn_Wo': _L0_xattn_in['Wo'], 'L0_xattn_bo': _L0_xattn_in['bo'], 'L0_ffn_gate_weight': _L0_ffn_in['gate_weight'], 'L0_ffn_expert_up': _L0_ffn_in['expert_up'], 'L0_ffn_expert_down': _L0_ffn_in['expert_down'], 'L0_ffn_shared_up': _L0_ffn_in['shared_up'], 'L0_ffn_shared_down': _L0_ffn_in['shared_down'], 'L1_xattn_wq': _L1_xattn_in['wq'], 'L1_xattn_bq': _L1_xattn_in['bq'], 'L1_xattn_wk': _L1_xattn_in['wk'], 'L1_xattn_bk': _L1_xattn_in['bk'], 'L1_xattn_wv': _L1_xattn_in['wv'], 'L1_xattn_bv': _L1_xattn_in['bv'], 'L1_xattn_wo': _L1_xattn_in['wo'], 'L1_xattn_bo': _L1_xattn_in['bo'], 'L1_ffn_router_w': _L1_ffn_in['router_w'], 'L1_ffn_w1': _L1_ffn_in['w1'], 'L1_ffn_b1': _L1_ffn_in['b1'], 'L1_ffn_w2': _L1_ffn_in['w2'], 'L1_ffn_b2': _L1_ffn_in['b2'], 'L2_xattn_Wq': _L2_xattn_in['Wq'], 'L2_xattn_bq': _L2_xattn_in['bq'], 'L2_xattn_Wk': _L2_xattn_in['Wk'], 'L2_xattn_bk': _L2_xattn_in['bk'], 'L2_xattn_Wv': _L2_xattn_in['Wv'], 'L2_xattn_bv': _L2_xattn_in['bv'], 'L2_xattn_Wo': _L2_xattn_in['Wo'], 'L2_xattn_bo': _L2_xattn_in['bo'], 'L2_ffn_Wg': _L2_ffn_in['Wg'], 'L2_ffn_bg': _L2_ffn_in['bg'], 'L2_ffn_We': _L2_ffn_in['We'], 'L2_ffn_be': _L2_ffn_in['be'], 'L3_xattn_Wq': _L3_xattn_in['Wq'], 'L3_xattn_Wk': _L3_xattn_in['Wk'], 'L3_xattn_Wv': _L3_xattn_in['Wv'], 'L3_xattn_Wo': _L3_xattn_in['Wo'], 'L3_ffn_router_w': _L3_ffn_in['router_w'], 'L3_ffn_router_b': _L3_ffn_in['router_b'], 'L3_ffn_w_gate': _L3_ffn_in['w_gate'], 'L3_ffn_w_up': _L3_ffn_in['w_up'], 'L3_ffn_w_down': _L3_ffn_in['w_down'], 'L3_ffn_sw_gate': _L3_ffn_in['sw_gate'], 'L3_ffn_sw_up': _L3_ffn_in['sw_up'], 'L3_ffn_sw_down': _L3_ffn_in['sw_down']}

def reference(x, ctx_768, mask_BxS2_bf1, L0_xattn_Wq, L0_xattn_bq, L0_xattn_Wkv, L0_xattn_bkv, L0_xattn_Wo, L0_xattn_bo, L0_ffn_gate_weight, L0_ffn_expert_up, L0_ffn_expert_down, L0_ffn_shared_up, L0_ffn_shared_down, L1_xattn_wq, L1_xattn_bq, L1_xattn_wk, L1_xattn_bk, L1_xattn_wv, L1_xattn_bv, L1_xattn_wo, L1_xattn_bo, L1_ffn_router_w, L1_ffn_w1, L1_ffn_b1, L1_ffn_w2, L1_ffn_b2, L2_xattn_Wq, L2_xattn_bq, L2_xattn_Wk, L2_xattn_bk, L2_xattn_Wv, L2_xattn_bv, L2_xattn_Wo, L2_xattn_bo, L2_ffn_Wg, L2_ffn_bg, L2_ffn_We, L2_ffn_be, L3_xattn_Wq, L3_xattn_Wk, L3_xattn_Wv, L3_xattn_Wo, L3_ffn_router_w, L3_ffn_router_b, L3_ffn_w_gate, L3_ffn_w_up, L3_ffn_w_down, L3_ffn_sw_gate, L3_ffn_sw_up, L3_ffn_sw_down):
    import jax
    import jax.numpy as jnp

    def _L0_xattn_ref(x, y, Wq, bq, Wkv, bkv, Wo, bo):
        import jax, jax.numpy as jnp
        import numpy as np
        N_HEADS = 16
        b, l, d = x.shape
        m = y.shape[1]
        h = N_HEADS
        dh = d // h
        q = (jnp.einsum('bld,ed->ble', x, Wq) + bq).reshape(b, l, h, dh)
        kv = (jnp.einsum('bmc,ec->bme', y, Wkv) + bkv).reshape(b, m, h, 2 * dh)
        k, v = (kv[..., :dh], kv[..., dh:])
        scale = 1.0 / jnp.sqrt(jnp.asarray(dh, x.dtype))
        att = jax.nn.softmax(jnp.einsum('blhd,bmhd->blmh', q, k) * scale, axis=2)
        out = jnp.einsum('blmh,bmhd->blhd', att, v).reshape(b, l, d)
        return jnp.einsum('bld,ed->ble', out, Wo) + bo

    def _L0_ffn_ref(hidden_states, gate_weight, expert_up, expert_down, shared_up, shared_down):
        import jax, jax.numpy as jnp
        import numpy as np
        TOP_K = 4
        N_GROUP = 4
        TOPK_GROUP = 2
        ROUTED_SCALING = 2.5

        def _route(x, gate_weight):
            scores = jax.nn.sigmoid(x @ gate_weight.T)
            T, E = scores.shape
            gs = E // N_GROUP
            top2, _ = jax.lax.top_k(scores.reshape(T, N_GROUP, gs), 2)
            group_scores = top2.sum(-1)
            _, gidx = jax.lax.top_k(group_scores, TOPK_GROUP)
            gmask = jax.nn.one_hot(gidx, N_GROUP, dtype=jnp.float32).sum(1)
            smask = jnp.repeat(gmask, gs, axis=1) > 0.5
            masked = jnp.where(smask, scores, 0.0)
            topk_idx = jax.lax.top_k(masked, TOP_K)[1]
            topk_w = jnp.take_along_axis(scores, topk_idx, axis=1)
            topk_w = topk_w / (topk_w.sum(-1, keepdims=True) + 1e-20)
            topk_w = topk_w * ROUTED_SCALING
            combine = jnp.zeros((T, E), jnp.float32).at[jnp.arange(T)[:, None], topk_idx].add(topk_w)
            return combine
        B, S, H = hidden_states.shape
        x = hidden_states.reshape(-1, H)
        combine = _route(x.astype(jnp.float32), gate_weight)
        up = jnp.einsum('th,ehi->eti', x, expert_up)
        down = jnp.einsum('eti,eih->eth', jax.nn.silu(up), expert_down)
        moe_out = jnp.einsum('te,eth->th', combine, down)
        shared = jax.nn.silu(x @ shared_up) @ shared_down
        return (moe_out + shared).reshape(B, S, H)

    def _L1_xattn_ref(x, y, wq, bq, wk, bk, wv, bv, wo, bo):
        import jax, jax.numpy as jnp
        import numpy as np
        N_HEADS = 16
        DIM_EMBED = 256
        DIM_CROSS = 192
        DIM_HEAD = DIM_EMBED // N_HEADS
        B, Sq, E = x.shape
        H, D = (N_HEADS, DIM_HEAD)
        q = (x @ wq + bq).reshape(B, Sq, H, D).transpose(0, 2, 1, 3)
        k = (y @ wk + bk).reshape(B, -1, H, D).transpose(0, 2, 1, 3)
        v = (y @ wv + bv).reshape(B, -1, H, D).transpose(0, 2, 1, 3)
        scores = jnp.einsum('bhqd,bhkd->bhqk', q, k) / jnp.sqrt(jnp.asarray(D, x.dtype))
        attn = jax.nn.softmax(scores, axis=-1)
        out = jnp.einsum('bhqk,bhkd->bhqd', attn, v)
        out = out.transpose(0, 2, 1, 3).reshape(B, Sq, E)
        return out @ wo + bo

    def _L1_ffn_ref(hidden_states, router_w, w1, b1, w2, b2):
        import jax, jax.numpy as jnp
        import numpy as np
        TOP_K = 2
        x = hidden_states
        router_logits = jnp.einsum('bth,eh->bte', x, router_w)
        topk_values, topk_indices = jax.lax.top_k(router_logits, TOP_K)
        topk_weights = jax.nn.softmax(topk_values.astype(jnp.float32), axis=-1).astype(x.dtype)
        h1 = jnp.einsum('bth,efh->btef', x, w1) + b1
        h1 = jax.nn.gelu(h1, approximate=False)
        expert_outputs = jnp.einsum('btef,ehf->bteh', h1, w2) + b2
        gather_idx = topk_indices[..., None]
        topk_expert_outputs = jnp.take_along_axis(expert_outputs, gather_idx, axis=2)
        mixed_output = jnp.sum(topk_expert_outputs * topk_weights[..., None], axis=2)
        return mixed_output

    def _L2_xattn_ref(x, y, Wq, bq, Wk, bk, Wv, bv, Wo, bo):
        import jax, jax.numpy as jnp
        import numpy as np
        import math
        N_HEADS = 8
        D_EMBED = 256
        D_CROSS = 192
        D_HEAD = D_EMBED // N_HEADS
        B, S, _ = x.shape
        SKV = y.shape[1]
        q = x @ Wq.T + bq
        k = y @ Wk.T + bk
        v = y @ Wv.T + bv
        q = q.reshape(B, S, N_HEADS, D_HEAD).transpose(0, 2, 1, 3)
        k = k.reshape(B, SKV, N_HEADS, D_HEAD).transpose(0, 2, 1, 3)
        v = v.reshape(B, SKV, N_HEADS, D_HEAD).transpose(0, 2, 1, 3)
        scores = jnp.einsum('bhqd,bhkd->bhqk', q, k) / math.sqrt(D_HEAD)
        attn = jax.nn.softmax(scores, axis=-1)
        out = jnp.einsum('bhqk,bhkd->bhqd', attn, v)
        out = out.transpose(0, 2, 1, 3).reshape(B, S, D_EMBED)
        return out @ Wo.T + bo

    def _L2_ffn_ref(x, Wg, bg, We, be):
        import jax, jax.numpy as jnp
        import numpy as np
        IN_DIM = 256
        OUT_DIM = 256
        NUM_EXPERTS = 8
        TOP_K = 2
        gate = jax.nn.softmax(x @ Wg + bg, axis=-1)
        topk_vals, topk_idx = jax.lax.top_k(gate, TOP_K)
        onehot = jax.nn.one_hot(topk_idx, NUM_EXPERTS, dtype=gate.dtype)
        gate_sparse = jnp.einsum('bsk,bske->bse', topk_vals, onehot)
        gate_sparse = gate_sparse / jnp.sum(gate_sparse, axis=-1, keepdims=True)
        y = jnp.einsum('bsi,eoi->bseo', x, We) + be[None, None, :, :].transpose(0, 1, 2, 3)
        out = jnp.einsum('bseo,bse->bso', y, gate_sparse)
        return out

    def _L3_xattn_ref(x, context, context_mask, Wq, Wk, Wv, Wo):
        import jax, jax.numpy as jnp
        import numpy as np
        DIM = 256
        CTX_DIM = 192
        HEADS = 16
        B, N, _ = x.shape
        M = context.shape[1]
        hd = DIM // HEADS
        scale = hd ** (-0.5)
        q = (x @ Wq).reshape(B, N, HEADS, hd).transpose(0, 2, 1, 3)
        k = (context @ Wk).reshape(B, M, HEADS, hd).transpose(0, 2, 1, 3)
        v = (context @ Wv).reshape(B, M, HEADS, hd).transpose(0, 2, 1, 3)
        scores = jnp.einsum('bhid,bhjd->bhij', q, k) * scale
        max_neg = -jnp.finfo(scores.dtype).max
        scores = jnp.where(context_mask[:, None, None, :], scores, max_neg)
        attn = jax.nn.softmax(scores, axis=-1)
        out = jnp.einsum('bhij,bhjd->bhid', attn, v)
        out = out.transpose(0, 2, 1, 3).reshape(B, N, DIM)
        return out @ Wo

    def _L3_ffn_ref(x, router_w, router_b, w_gate, w_up, w_down, sw_gate, sw_up, sw_down):
        import jax, jax.numpy as jnp
        import numpy as np
        B, S, D = (1, 512, 256)
        F = 352
        E = 16
        K = 2
        CAP_FACTOR = 1.25

        def _mlp(h, wg, wu, wd):
            return jax.nn.silu(h @ wg) * (h @ wu) @ wd
        b, s, d = x.shape
        N = b * s
        NK = N * K
        C = int(np.ceil(CAP_FACTOR * NK / E))
        x_tokens = x.reshape(N, d)
        logits = x_tokens @ router_w + router_b
        probs = jax.nn.softmax(logits, axis=-1)
        vals, idx = jax.lax.top_k(probs, K)
        vals = vals / (jnp.sum(vals, axis=-1, keepdims=True) + 1e-09)
        idx_flat = idx.reshape(NK)
        vals_flat = vals.reshape(NK)
        oh_e = jax.nn.one_hot(idx_flat, E, dtype=x.dtype)
        pos = (jnp.cumsum(oh_e, axis=0) * oh_e).sum(axis=1) - 1
        within = (pos < C).astype(x.dtype)
        pos_c = jnp.clip(pos, 0, C - 1).astype(jnp.int32)
        token_ids = jnp.arange(NK) // K
        x_pair = x_tokens[token_ids] * within[:, None]
        expert_inputs = jnp.zeros((E, C, d), x.dtype).at[idx_flat, pos_c].add(x_pair)
        expert_outputs = jax.vmap(_mlp)(expert_inputs, w_gate, w_up, w_down)
        gathered = expert_outputs[idx_flat, pos_c] * (vals_flat * within)[:, None]
        output_tokens = gathered.reshape(N, K, d).sum(axis=1)
        return x + _mlp(x, sw_gate, sw_up, sw_down) + output_tokens.reshape(b, s, d)
    x = x + _L0_xattn_ref(_layernorm(x, axis=-1), ctx_768, L0_xattn_Wq, L0_xattn_bq, L0_xattn_Wkv, L0_xattn_bkv, L0_xattn_Wo, L0_xattn_bo)
    x = x + _L0_ffn_ref(_layernorm(x, axis=-1), L0_ffn_gate_weight, L0_ffn_expert_up, L0_ffn_expert_down, L0_ffn_shared_up, L0_ffn_shared_down)
    x = x + _L1_xattn_ref(_layernorm(x, axis=-1), ctx_768, L1_xattn_wq, L1_xattn_bq, L1_xattn_wk, L1_xattn_bk, L1_xattn_wv, L1_xattn_bv, L1_xattn_wo, L1_xattn_bo)
    x = x + _L1_ffn_ref(_layernorm(x, axis=-1), L1_ffn_router_w, L1_ffn_w1, L1_ffn_b1, L1_ffn_w2, L1_ffn_b2)
    x = x + _L2_xattn_ref(_layernorm(x, axis=-1), ctx_768, L2_xattn_Wq, L2_xattn_bq, L2_xattn_Wk, L2_xattn_bk, L2_xattn_Wv, L2_xattn_bv, L2_xattn_Wo, L2_xattn_bo)
    x = x + _L2_ffn_ref(_layernorm(x, axis=-1), L2_ffn_Wg, L2_ffn_bg, L2_ffn_We, L2_ffn_be)
    x = x + _L3_xattn_ref(_layernorm(x, axis=-1), ctx_768, mask_BxS2_bf1, L3_xattn_Wq, L3_xattn_Wk, L3_xattn_Wv, L3_xattn_Wo)
    x = x + _L3_ffn_ref(_layernorm(x, axis=-1), L3_ffn_router_w, L3_ffn_router_b, L3_ffn_w_gate, L3_ffn_w_up, L3_ffn_w_down, L3_ffn_sw_gate, L3_ffn_sw_up, L3_ffn_sw_down)
    return x

_drawn_inputs = setup_inputs


def setup_inputs(seed=0):
    import zlib

    import numpy as np

    out = dict(_drawn_inputs(seed))
    spreads = {'L2_xattn_bq': (0.0, 0.279),
     'L2_xattn_bk': (0.0, 0.8),
     'L2_xattn_bv': (0.0, 0.1),
     'L2_xattn_bo': (0.0, 0.1),
     'L2_ffn_bg': (0.0, 0.1),
     'L3_ffn_router_b': (0.0, 0.8)}
    factors = {'L0_xattn_bq': 6.869,
     'L0_xattn_bo': 3.073,
     'L1_xattn_bq': 8.0,
     'L1_xattn_bk': 8.0,
     'L1_xattn_bv': 4.324,
     'L1_xattn_bo': 3.496,
     'L1_ffn_b1': 6.342,
     'L1_ffn_b2': 2.798,
     'L2_ffn_be': 3.356,
     'L3_ffn_router_w': 8.0,
     'L3_ffn_w_gate': 8.0,
     'L3_ffn_w_up': 8.0,
     'L3_ffn_w_down': 8.0,
     'L3_ffn_sw_gate': 6.746,
     'L3_ffn_sw_up': 6.909,
     'L3_ffn_sw_down': 6.994}
    for name, (base, spread) in spreads.items():
        noise = np.random.default_rng([zlib.crc32(name.encode()), seed]).standard_normal(out[name].shape)
        drawn = base * np.exp(spread * noise) if base else spread * noise
        out[name] = jnp.asarray(drawn.astype(out[name].dtype))
    for name, factor in factors.items():
        out[name] = (out[name] * factor).astype(out[name].dtype)
    return out
```

```python
import concourse.bass as bass
from concourse import mybir
from contextlib import ExitStack

T, D, S, DC = 2048, 256, 1601, 192
P = 128
NT = T // P
Q = 512
NQ = T // Q
TPQ = Q // P
NK = (S + P - 1) // P
KREM = S - (NK - 1) * P
NG = 4
CK = [401, 400, 400, 400]
CKO = [0, 401, 801, 1201]
MASKED = -float(2.0 ** 127)
CAP = 320
CT = (CAP + P - 1) // P
CLAST = CAP - (CT - 1) * P
PLACES = 16 * CAP
EPS = 1e-5

ATT = [dict(dh=16, pw=32, hpg=4, nsub=1), dict(dh=16, pw=32, hpg=4, nsub=1),
       dict(dh=32, pw=64, hpg=2, nsub=2), dict(dh=16, pw=32, hpg=4, nsub=1)]
FFN = [dict(E=16, EA=20, ft=[128], gated=False, topk=4),
       dict(E=8, EA=8, ft=[128] * 8, gated=False, topk=2),
       dict(E=8, EA=8, ft=[], gated=False, topk=2),
       dict(E=16, EA=17, ft=[128, 128, 96], gated=True, topk=2)]


class Count:

    def __init__(self, sem, n=0):
        self.sem, self.n, self.it, self.per, self.first = sem, n, None, 0, 0

    def loop(self, it, first, per):
        self.it, self.first, self.per, self.start = it, first, per, self.n

    def end(self, trips):
        assert self.n - self.start == self.per, (self.sem, self.n - self.start, self.per)
        self.n, self.it = self.start + trips * self.per, None

    def step(self, more=1):
        self.n += more

    def at(self, back=0):
        v = self.n - back
        assert v > 0, self.sem
        return v if self.it is None or self.per == 0 else (self.it - self.first) * self.per + v


def chunk_of(n, parts):
    return [n * i // parts for i in range(parts + 1)]


def side_schedule(g, hpg, first, last):
    units = hpg * TPQ
    nxt1 = not (last and g == NG - 1)
    nxt2 = not (last and g >= NG - 2)
    half = units // 2
    late = [("max", (g + 1) % NG, u, c) for u in range(half, units) for c in range(4)] if nxt1 else []
    early = [("max", (g + 2) % NG, u, c) for u in range(half) for c in range(4)] if nxt2 else []
    jobs = late + early[:6] + ([("turn", (g + 1) % NG)] if nxt1 else []) + early[6:]
    cut = chunk_of(len(jobs), NK)
    slots = [jobs[cut[k]:cut[k + 1]] for k in range(NK)]
    if not (first and g == 0):
        slots[2].append(("den", (g - 1) % NG))
        slots[5].append(("spread", (g - 1) % NG))
        if g == 0:
            for i in range(TPQ):
                slots[6 + i].append(("out", i))
    return slots


def max_jobs(g, hpg, lo, hi):
    return [("max", g, u, c) for u in range(lo, hi) for c in range(4)]


def side_prologue(hpg):
    units = hpg * TPQ
    return max_jobs(0, hpg, 0, units) + [("turn", 0)] + max_jobs(1, hpg, 0, units // 2)


def build(nc, A, out):
    f32, bf16, u8, u32 = mybir.dt.float32, mybir.dt.bfloat16, mybir.dt.uint8, mybir.dt.uint32
    ALU, ACT, AX = mybir.AluOpType, mybir.ActivationFunctionType, mybir.AxisListType

    q_parts = nc.dram_tensor("q_parts", [3, D, T], bf16, kind="Internal").ap()
    k_parts = nc.dram_tensor("k_parts", [3, D, S], bf16, kind="Internal").ap()
    x_place = nc.dram_tensor("x_place", [PLACES, D], f32, kind="Internal").ap()
    y_place = nc.dram_tensor("y_place", [PLACES, D], f32, kind="Internal").ap()
    m_parts = nc.dram_tensor("m_parts", [4, NG * TPQ * P], bf16, kind="Internal").ap()

    ctx = ExitStack()
    with ctx:
        def sb(name, shape, dt=f32, stack=ctx):
            return stack.enter_context(nc.sbuf_tensor(name, shape, dt))

        def sem(name):
            return ctx.enter_context(nc.semaphore(name))

        X = sb("x_res", [P, NT, D])
        xnT = sb("xn_t", [P, 2, T])
        C0 = sb("ctx_a", [P, S])
        C1 = sb("ctx_b", [DC - P + 1, S])
        ident = sb("ident", [P, P])
        sel16 = sb("sel16", [P, 4])
        sel32 = sb("sel32", [P, 4])
        mask_u8 = sb("mask_u8", [P, NK], u8)
        mask_row_u8 = sb("mask_row_u8", [1, S], u8)
        mask_col = sb("mask_col", [P, NK])
        mask_row = sb("mask_row", [1, S], bf16)
        zero_col = sb("zero_col", [P, 1])
        ones_row = sb("ones_row", [1, 4, Q], bf16)
        stat = sb("stat", [P, NT, 6])
        mv = sb("mv", [P, NT, 2])
        rstd = sb("rstd", [P, NT])
        WQ = sb("wq", [P, 2, D])
        BQ = sb("bq", [P, 2])
        WK0 = sb("wk0", [P, D])
        WK1 = sb("wk1", [DC - P + 1, D])
        WV0 = sb("wv0", [P, 512])
        WV1 = sb("wv1", [DC - P + 1, 512])
        WO = sb("wo", [P, NG, D])

        att = ExitStack()
        with att:
            KS = sb("k_stack", [100, 16, S], bf16, att)
            V = sb("v", [P, NK, 512], f32, att)
            PR = [sb(f"probs{i}", [P, 2, Q], f32, att) for i in range(4)]
            QS = [sb(f"q_stack{i}", [100, 4, Q], bf16, att) for i in range(4)]
            OS = [sb(f"o_sum{i}", [P, Q], f32, att) for i in range(2)]
            RD = sb("recip", [P, 16], f32, att)
            RDX = sb("recip_wide", [P, Q], f32, att)
            OT = sb("o_t", [P, NG, Q], f32, att)
            MX4 = [sb(f"mx4_{i}", [P, 16, 4], f32, att) for i in range(2)]
            MX = [sb(f"mx{i}", [P, 16], f32, att) for i in range(2)]
            MN = sb("m_neg", [16, P], f32, att)
            MR = sb("m_rest", [16, P], f32, att)
            MP = sb("m_part", [16, 4, P], bf16, att)
        prj = ExitStack()
        with prj:
            sb("skip", [100, 16, S], bf16, prj)
            sb("skip_v", [P, NK, 512], f32, prj)
            QK = [sb(f"qk{i}", [P, Q], f32, prj) for i in range(2)]
            QR = [sb(f"qk_rest{i}", [P, Q], f32, prj) for i in range(2)]
            QP = [sb(f"qk_part{i}", [P, 3, Q], bf16, prj) for i in range(2)]
        ffn = ExitStack()
        with ffn:
            XN = sb("xn", [P, NT, D], f32, ffn)
            WU = [sb(f"w_up{i}", [P, 2 * 1024], f32, ffn) for i in range(2)]
            WD = [sb(f"w_down{i}", [P, 8, D], f32, ffn) for i in range(2)]
            B1 = [sb(f"b1_{i}", [P, 8], f32, ffn) for i in range(2)]
            HT = [sb(f"h_t{i}", [P, 8, Q], f32, ffn) for i in range(2)]
            SG = [sb(f"silu_gate{i}", [P, Q], f32, ffn) for i in range(2)]
            GW = sb("gate_w", [P, 2, 16], f32, ffn)
            GB = sb("gate_b", [P, 16], f32, ffn)
            B2 = sb("b2", [8, D], f32, ffn)
            combT = sb("comb_t", [8, T], f32, ffn)
            LG = sb("logits", [P, NT, 16], f32, ffn)
            PB = sb("prob", [P, NT, 16], f32, ffn)
            SL = sb("sel", [P, NT, 16], f32, ffn)
            MK = sb("masked", [P, NT, 16], f32, ffn)
            RK = sb("rank", [P, NT, 16], f32, ffn)
            T4 = [sb(f"t4_{i}", [P, NT, 4], f32, ffn) for i in range(6)]
            R1 = sb("r1", [P, NT], f32, ffn)
            R2 = sb("r2", [P, NT], f32, ffn)
            BIG = [sb(f"big{i}", [P, 4, 16, 16], f32, ffn) for i in range(2)]
            comb = sb("comb", [P, NT, 20], f32, ffn)
            less = sb("less", [P, 16, 16], f32, ffn)
            tri = sb("tri", [P, P], f32, ffn)
            ones = sb("ones", [P, P], f32, ffn)
            TOT = sb("totals", [P, NT + 1, 16], f32, ffn)
            POS = sb("place", [P, NT, 16], f32, ffn)
            WI = sb("within", [P, NT, 16], f32, ffn)
            first_place = sb("first_place", [P, 16], f32, ffn)
            WR = [sb(f"weight_rank{r}", [P, NT], f32, ffn) for r in range(2)]
            IP = [sb(f"place_rank{r}", [P, NT], f32, ffn) for r in range(2)]
            IS = [sb(f"scatter_rank{r}", [P, NT], u32, ffn) for r in range(2)]
            IG = [sb(f"gather_rank{r}", [P, NT], u32, ffn) for r in range(2)]
            XE = [sb(f"x_expert{i}", [P, CT, D], f32, ffn) for i in range(2)]
            XT = [sb(f"x_expert_t{i}", [P, 2, CAP], f32, ffn) for i in range(2)]
            YE = [sb(f"y_expert{i}", [P, CT, D], f32, ffn) for i in range(2)]
            YG = [sb(f"y_token{i}", [P, D], f32, ffn) for i in range(4)]

        PS = ctx.enter_context(nc.psum_tensor("ps", [P, 8, 512], f32))

        s_fence = sem("s_fence")
        s_in = sem("s_in")
        s_const = sem("s_const")
        s_wpad = sem("s_wpad")
        s_wa = sem("s_wa")
        s_stat = sem("s_stat")
        s_std = sem("s_std")
        s_xn = sem("s_xn")
        s_xt = sem("s_xt")
        s_xtc = sem("s_xtc")
        s_v = sem("s_v")
        s_pj = sem("s_pj")
        s_pc = sem("s_pc")
        s_p1 = sem("s_p1")
        s_pp = sem("s_pp")
        s_pd = [sem(f"s_pd{i}") for i in range(2)]
        s_vj = sem("s_vj")
        s_vc = sem("s_vc")
        s_ks = sem("s_ks")
        s_kst = sem("s_kst")
        s_ql = [sem(f"s_ql{i}") for i in range(4)]
        s_md = sem("s_md")
        s_mr = sem("s_mr")
        s_sc = sem("s_sc")
        s_pr = sem("s_pr")
        s_pv = sem("s_pv")
        s_os = sem("s_os")
        s_ot = sem("s_ot")
        s_rd = sem("s_rd")
        s_rx = sem("s_rx")
        s_sj = sem("s_sj")
        s_sf = sem("s_sf")
        s_mx = sem("s_mx")
        s_mp = sem("s_mp")
        s_gl = sem("s_gl")
        s_lg = sem("s_lg")
        s_lc = sem("s_lc")
        s_ex = sem("s_ex")
        s_cb = sem("s_cb")
        s_ct = sem("s_ct")
        s_ctc = sem("s_ctc")
        s_by = sem("s_by")
        s_w = [sem(f"s_w{i}") for i in range(2)]
        s_h = sem("s_h")
        s_sg = sem("s_sg")
        s_hr = sem("s_hr")
        s_y = sem("s_y")
        s_yf = sem("s_yf")
        s_z = sem("s_z")
        s_ix = sem("s_ix")
        s_px = sem("s_px")
        s_xe = [sem(f"s_xe{i}") for i in range(2)]
        s_tr = sem("s_tr")
        s_te = sem("s_te")
        s_yc = sem("s_yc")
        s_yd = [sem(f"s_yd{i}") for i in range(2)]
        s_yg = [sem(f"s_yg{i}") for i in range(4)]
        s_out = sem("s_out")

        HR_FREE, YF_FREE, Y_FREE = 4, 4, 2 * TPQ

        block = ctx.enter_context(nc.Block())

        def fence(eng, n):
            n[0] += 1
            eng.drain().then_inc(s_fence, 1)
            eng.wait_ge(s_fence, 5 * n[0])

        def key_rows(k):
            return P if k < NK - 1 else KREM

        @block.sync
        def _(sp):
            fences = [0]
            wpad, kst, pp = Count(s_wpad), Count(s_kst), Count(s_pp)
            pd = [Count(s) for s in s_pd]
            mp, md, pv = Count(s_mp), Count(s_md), Count(s_pv)
            wf = Count(s_y, Y_FREE)
            px, yc, tr = Count(s_px), Count(s_yc), Count(s_tr)

            def load_attention_weights(L):
                a = ATT[L]
                dh, pw, hpg = a["dh"], a["pw"], a["hpg"]
                H = D // dh
                n = 0
                wpad.step()
                sp.wait_ge(s_wpad, wpad.at())
                loads = [(WQ[:], A[f"wq{L}"].rearrange("(k p) n -> p k n", p=P)),
                         (WK0[:], A[f"wk{L}"][0:P, :]), (WK1[0:DC - P, :], A[f"wk{L}"][P:DC, :]),
                         (WV0[:].rearrange("p (h w) -> p h w", w=pw)[:, :, 0:dh],
                          A[f"wv{L}"][0:P, :].rearrange("p (h w) -> p h w", w=dh)),
                         (WV1[0:DC - P, :].rearrange("p (h w) -> p h w", w=pw)[:, :, 0:dh],
                          A[f"wv{L}"][P:DC, :].rearrange("p (h w) -> p h w", w=dh))]
                for j in range(hpg):
                    loads.append((WO[pw * j:pw * j + dh, :, :],
                                  A[f"wo{L}"].rearrange("(g j d) n -> j d g n", g=NG, j=hpg)[j]))
                if L < 3:
                    loads += [(BQ[:], A[f"bq{L}"].rearrange("(m p) -> p m", p=P)),
                              (WK1[DC - P:DC - P + 1, :], A[f"bk{L}"].rearrange("(a n) -> a n", a=1)),
                              (WV1[DC - P:DC - P + 1, :].rearrange("p (h w) -> p h w", w=pw)[:, :, 0:dh],
                               A[f"bv{L}"].rearrange("(a h w) -> a h w", a=1, w=dh)),
                              (WO[dh:dh + 1, 0, :], A[f"bo{L}"].rearrange("(a n) -> a n", a=1))]
                for dst, src in loads:
                    sp.dma_start(dst, src, allow_slow_non_contiguous=True).then_inc(s_wa, 16)

            def load_queries(L, t, buf):
                a = ATT[L]
                dh, hpg = a["dh"], a["hpg"]
                c, g = (t, 0) if isinstance(t, int) else t
                cols = bass.ts(c, Q)
                dst = QS[buf]
                if a["nsub"] == 1:
                    for row, part in enumerate([0, 0, 0, 1, 1, 2]):
                        src = q_parts[part].rearrange("(h d) t -> d h t", d=dh)[:, g * hpg:(g + 1) * hpg, cols]
                        sp.dma_start(dst[row * dh:(row + 1) * dh, :, :], src).then_inc(s_ql[buf], 16)
                else:
                    for row, part in enumerate([0, 0, 0, 1, 1, 2]):
                        src = q_parts[part].rearrange("(h d) t -> d h t", d=dh)[:, g * hpg:(g + 1) * hpg, cols]
                        r = row % 3
                        sp.dma_start(dst[r * dh:(r + 1) * dh, row // 3::2, :], src).then_inc(s_ql[buf], 16)
                sp.dma_start(dst[96:97, :, :], ones_row[:]).then_inc(s_ql[buf], 16)

            def store_max_rows(L, g):
                a = ATT[L]
                units = a["hpg"] * TPQ
                mp.step()
                sp.wait_ge(s_mp, mp.at())
                m_dst = m_parts[:, 0:units * P].rearrange("r (u x) -> u r x", u=units)
                sp.dma_start(m_dst, MP[0:units, :, :]).then_inc(s_md, 16)
                md.step(16)
                if md.n > 0:
                    sp.wait_ge(s_md, md.at())
                src = m_parts[:, 0:units * P].rearrange("r (j x) -> r j x", x=Q)
                sp.dma_start(QS[g][96:100, 0:4:a["nsub"], :], src).then_inc(s_mr, 16)

            sp.dma_start(X[:], A["x"].rearrange("(t p) d -> p t d", p=P)).then_inc(s_in, 16)
            sp.dma_start(C0[:], A["ctx_t"][0:P, :]).then_inc(s_in, 16)
            sp.dma_start(C1[0:DC - P, :], A["ctx_t"][P:DC, :]).then_inc(s_in, 16)
            sp.dma_start(mask_u8[:, 0:NK - 1], A["mask"][:, 0:P * (NK - 1)].rearrange("a (k p) -> p (a k)", p=P),
                         allow_slow_non_contiguous=True).then_inc(s_in, 16)
            sp.dma_start(mask_u8[0:KREM, NK - 1:NK], A["mask"][:, P * (NK - 1):S].rearrange("a p -> p a"),
                         allow_slow_non_contiguous=True).then_inc(s_in, 16)
            sp.dma_start(mask_row_u8[:], A["mask"]).then_inc(s_in, 16)
            load_attention_weights(0)
            fence(sp, fences)

            for L in range(4):
                a = ATT[L]
                fence(sp, fences)
                for u in range(16):
                    kind, m, c = u // 8, (u // 4) % 2, u % 4
                    pp.step()
                    sp.wait_ge(s_pp, pp.at())
                    n = Q if kind == 0 else min(Q, S - c * Q)
                    where = q_parts if kind == 0 else k_parts
                    dst = where[:, m * P:(m + 1) * P, c * Q:c * Q + n].rearrange("r p t -> p r t")
                    sp.dma_start(dst, QP[u % 2][:, :, 0:n]).then_inc(s_pd[u % 2], 16)
                    pd[u % 2].step(16)
                for i in range(2):
                    sp.wait_ge(s_pd[i], pd[i].at())
                dh = a["dh"]
                kst.step()
                sp.wait_ge(s_kst, kst.at())
                kp = k_parts.rearrange("r (h d) s -> r d h s", d=dh)
                for row, part in enumerate([0, 1, 2, 0, 1, 0]):
                    if a["nsub"] == 1:
                        dst = KS[row * dh:(row + 1) * dh, :, :]
                    else:
                        dst = KS[(row % 3) * dh:(row % 3 + 1) * dh, row // 3::2, :]
                    sp.dma_start(dst, kp[part]).then_inc(s_ks, 16)
                if L == 3:
                    for h in range(16):
                        sp.dma_start(KS[96:97, h, :], mask_row[:]).then_inc(s_ks, 16)
                fence(sp, fences)

                for g in range(3):
                    load_queries(L, (0, g), g)
                store_max_rows(L, 0)

                pairs = NK * a["hpg"] // 2

                def iteration(it, first, last):
                    for g in range(NG):
                        if not (first and g == 0):
                            pv.step(pairs)
                        if not (last and g > 0):
                            if not (first and g == 0):
                                sp.wait_ge(s_pv, pv.at())
                            load_queries(L, (it, 3) if g == 0 else (it + 1, g - 1), (g + 3) % 4)
                        if not (last and g == NG - 1):
                            store_max_rows(L, (g + 1) % NG)

                iteration(0, True, False)
                with sp.Fori(1, NQ - 1) as it:
                    for c, per in ((mp, 4), (md, 64), (pv, NG * pairs)):
                        c.loop(it, 1, per)
                    iteration(it, False, False)
                    for c in (mp, md, pv):
                        c.end(NQ - 2)
                iteration(NQ - 1, False, True)
                pv.step(pairs)
                fence(sp, fences)

                f = FFN[L]
                E = f["E"]
                if L < 3:
                    load_attention_weights(L + 1)
                sp.dma_start(GW[:, :, 0:E], A[f"gw{L}"].rearrange("(k p) e -> p k e", p=P),
                             allow_slow_non_contiguous=True).then_inc(s_gl, 16)
                if L >= 2:
                    sp.dma_start(GB[:, 0:E], A[f"gb{L}"].partition_broadcast(P)).then_inc(s_gl, 16)
                if L in (1, 2):
                    sp.dma_start(B2[:], A[f"b2_{L}"]).then_inc(s_gl, 16)

                def load_expert(e, par):
                    def at(name):
                        return A[name][bass.ds(e, 1)].rearrange("a p x -> (a p) x")
                    if L == 2:
                        sp.dma_start(WU[par][:, 0:1024], at("we2")).then_inc(s_w[par], 16)
                        return
                    F = sum(f["ft"]) * (2 if f["gated"] else 1)
                    sp.dma_start(WU[par][:, 0:2 * F], at(f"up{L}")).then_inc(s_w[par], 16)
                    full = sum(1 for r in f["ft"] if r == P)
                    sp.dma_start(WD[par][:, 0:full, :].rearrange("p f n -> p (f n)"), at(f"down{L}")).then_inc(s_w[par], 16)
                    if f["gated"]:
                        sp.dma_start(WD[par][0:96, 2, :], at("down3b")).then_inc(s_w[par], 16)
                    if L == 1:
                        sp.dma_start(B1[par][:], at("b1")).then_inc(s_w[par], 16)

                items = f["EA"] if L != 2 else 4
                fence(sp, fences)
                if L < 3:
                    for par in range(2):
                        load_expert(par, par)
                    with sp.Fori(1, items // 2) as i:
                        wf.loop(i, 1, 2 * NT)
                        for par in range(2):
                            wf.step(NT)
                            sp.wait_ge(s_y, wf.at())
                            load_expert(i * 2 + par, par)
                        wf.end(items // 2 - 1)
                    wf.step(2 * NT)
                else:
                    load_expert(16, 0)
                    load_expert(0, 1)
                    px.step(2 * NT * 16)
                    sp.wait_ge(s_px, px.at())

                    def load_rows(e, par):
                        rows = x_place.rearrange("(e r) d -> e r d", r=CAP)[bass.ds(e, 1)].rearrange("a r d -> (a r) d")
                        full = (CT - 1) * P
                        sp.dma_start(XE[par][:, 0:CT - 1, :], rows[0:full, :].rearrange("(t p) d -> p t d", p=P))\
                          .then_inc(s_xe[par], 16)
                        sp.dma_start(XE[par][0:CLAST, CT - 1, :], rows[full:CAP, :]).then_inc(s_xe[par], 16)

                    def store_answers(e, par):
                        rows = y_place.rearrange("(e r) d -> e r d", r=CAP)[bass.ds(e, 1)].rearrange("a r d -> (a r) d")
                        full = (CT - 1) * P
                        sp.dma_start(rows[0:full, :].rearrange("(t p) d -> p t d", p=P), YE[par][:, 0:CT - 1, :])\
                          .then_inc(s_yd[par], 16)
                        sp.dma_start(rows[full:CAP, :], YE[par][0:CLAST, CT - 1, :]).then_inc(s_yd[par], 16)

                    load_rows(0, 0)
                    load_rows(1, 1)
                    wf.step(NT)
                    sp.wait_ge(s_y, wf.at())
                    load_expert(1, 0)

                    def turn(e, par):
                        yc.step(CT)
                        sp.wait_ge(s_yc, yc.at())
                        store_answers(e, par)

                    with sp.Fori(1, 8) as i:
                        loops = ((yc, 2 * CT), (tr, 2))
                        for c, per in loops:
                            c.loop(i, 1, per)
                        for par in range(2):
                            tr.step()
                            sp.wait_ge(s_tr, tr.at())
                            load_rows(i * 2 + par, par)
                            turn(i * 2 - 2 + par, par)
                            load_expert(i * 2 + par, 1 - par)
                        for c, per in loops:
                            c.end(7)
                    for par in range(2):
                        turn(14 + par, par)
                fence(sp, fences)
            sp.dma_start(out.rearrange("(t p) d -> p t d", p=P), X[:]).then_inc(s_out, 16)
            sp.wait_ge(s_out, 16)

        @block.gpsimd
        def _(pool):
            fences = [0]
            n = [0]

            def link(ins):
                n[0] += 1
                ins.then_inc(s_const, 1)
                pool.wait_ge(s_const, n[0])

            def clear_attention_weights(L):
                a = ATT[L]
                link(pool.memset(WV0[:], 0.0))
                link(pool.memset(WV1[:], 0.0))
                link(pool.memset(WK1[DC - P:DC - P + 1, :], 0.0))
                link(pool.memset(BQ[:], 0.0))
                v = WV1[DC - P:DC - P + 1, :].rearrange("p (h w) -> p h w", w=a["pw"])
                link(pool.memset(v[:, :, a["dh"]:a["dh"] + 1], 1.0))
                pool.memset(WO[:], 0.0).then_inc(s_wpad, 1)

            clear_attention_weights(0)
            link(pool.memset(zero_col[:], 0.0))
            link(pool.memset(ones_row[:], 1.0))
            link(pool.memset(C1[DC - P:DC - P + 1, :], 1.0))
            link(pool.memset(ident[:], 0.0))
            link(pool.affine_select(out=ident[:], in_=ident[:], compare_op=ALU.not_equal, fill=1.0,
                                    base=0, pattern=[[-1, P]], channel_multiplier=1))
            for m, pw, dh in ((sel16, 32, 16), (sel32, 64, 32)):
                link(pool.memset(m[:], 0.0))
                link(pool.affine_select(out=m[:], in_=m[:], compare_op=ALU.not_equal, fill=1.0, base=-dh,
                                        pattern=[[-pw, 4]], channel_multiplier=1))
            fence(pool, fences)
            for L in range(4):
                fence(pool, fences)
                link(pool.memset(KS[96:100, :, :], 1.0))
                link(pool.memset(KS[96:97, :, :], 0.0))
                pool.memset(MP[:, 0, :], 0.0).then_inc(s_kst, 1)
                fence(pool, fences)
                fence(pool, fences)
                if L < 3:
                    clear_attention_weights(L + 1)
                link(pool.memset(less[:], 1.0))
                link(pool.affine_select(out=less[:], in_=less[:], compare_op=ALU.is_gt, fill=0.0,
                                        base=0, pattern=[[1, 16], [-1, 16]], channel_multiplier=0))
                link(pool.memset(ones[:], 1.0))
                link(pool.affine_select(out=tri[:], in_=ones[:], compare_op=ALU.is_gt, fill=0.0,
                                        base=0, pattern=[[1, P]], channel_multiplier=-1))
                link(pool.memset(comb[:], 1.0))
                for e in range(16):
                    link(pool.memset(first_place[:, e:e + 1], float(CAP * e)))
                if L == 3:
                    link(pool.memset(YG[0][:], 0.0))
                    zeros = YG[0][:].unsqueeze(1).to_broadcast([P, PLACES // P, D])
                    pool.dma_start(x_place.rearrange("(a p) d -> p a d", p=P), zeros).then_inc(s_z, 16)
                fence(pool, fences)
                if L == 3:
                    pool.wait_ge(s_z, 16)
                    pool.wait_ge(s_ix, 1)
                    for r in range(2):
                        for t in range(NT):
                            pool.indirect_dma_start(x_place, bass.IndirectOffsetOnAxis(ap=IS[r][:, t:t + 1], axis=0),
                                                    XN[:, t, :], None, bounds_check=PLACES - 1,
                                                    oob_is_err=False).then_inc(s_px, 16)
                    for par in range(2):
                        pool.wait_ge(s_yd[par], 8 * 32)
                    for t in range(NT):
                        for r in range(2):
                            k = 2 * t + r
                            if k >= 4:
                                pool.wait_ge(s_ix, 1 + k - 3)
                            pool.indirect_dma_start(YG[k % 4][:], None, y_place,
                                                    bass.IndirectOffsetOnAxis(ap=IG[r][:, t:t + 1], axis=0))\
                                .then_inc(s_yg[k % 4], 16)
                fence(pool, fences)

        @block.scalar
        def _(act):
            act.sem_inc(s_hr, HR_FREE)
            act.sem_inc(s_yf, YF_FREE)
            act.sem_inc(s_y, Y_FREE)
            fences = [0]
            stat_c, xt, xtc = Count(s_stat), Count(s_xt), Count(s_xtc)
            pj, pp, pc = Count(s_pj), Count(s_pp), Count(s_pc)
            vj = Count(s_vj)
            sc, pv, o, ot, rd, dv = Count(s_sc), Count(s_pv), Count(s_pv), Count(s_ot), Count(s_rd), Count(s_ot)
            lc, ctc = Count(s_lc), Count(s_ct)
            h, dn, hr = Count(s_h), Count(s_y, Y_FREE), Count(s_hr, HR_FREE)
            tr = Count(s_tr)
            fence(act, fences)

            def normalize():
                stat_c.step()
                act.wait_ge(s_stat, stat_c.at())
                act.activation(rstd[:], mv[:, :, 1], ACT.Sqrt).then_inc(s_std, 1)
                for c in range(NQ):
                    xt.step()
                    act.wait_ge(s_xt, xt.at())
                    act.activation(xnT[:, 1, c * Q:(c + 1) * Q], PS[:, 1, :], ACT.Copy).then_inc(s_xtc, 1)
                fence(act, fences)

            for L in range(4):
                a = ATT[L]
                dh, pw, hpg, nsub = a["dh"], a["pw"], a["hpg"], a["nsub"]
                npair = hpg // 2
                normalize()

                scale = 0.25 if dh == 16 else 32.0 ** -0.5
                vq = []
                for u in range(16):
                    kind, m, c = u // 8, (u // 4) % 2, u % 4
                    n = Q if kind == 0 else min(Q, S - c * Q)
                    pj.step()
                    act.wait_ge(s_pj, pj.at())
                    if pp.n > 1:
                        act.wait_ge(s_pp, pp.at(1))
                    pp.step()
                    if kind == 0:
                        act.activation(QK[u % 2][:, 0:n], PS[:, u % 4, 0:n], ACT.Identity,
                                       bias=BQ[:, m:m + 1], scale=1.0).then_inc(s_pc, 1)
                    else:
                        act.activation(QK[u % 2][:, 0:n], PS[:, u % 4, 0:n], ACT.Copy).then_inc(s_pc, 1)
                    if u < NK:
                        vj.step()
                        act.wait_ge(s_vj, vj.at())
                        r = key_rows(u)
                        act.activation(V[0:r, u, :], PS[0:r, 4 + u % 4, :], ACT.Copy).then_inc(s_vc, 1)
                fence(act, fences)

                pair = [0]

                def exps(k):
                    r = key_rows(k)
                    bias = mask_col if L == 3 else None
                    for j in range(npair):
                        b = pair[0] % 2
                        sc.step()
                        act.wait_ge(s_sc, sc.at())
                        if pv.n > 3:
                            act.wait_ge(s_pv, pv.at(3))
                        pv.step()
                        act.activation(PR[pair[0] % 4][0:r, :, :], PS[0:r, 2 * b:2 * b + 2, :], ACT.Exp,
                                       bias=mask_col[0:r, k:k + 1] if L == 3 else zero_col[0:r, :],
                                       scale=1.0).then_inc(s_pr, 1)
                        pair[0] += 1

                def copy_sums(g):
                    o.step(NK * npair)
                    act.wait_ge(s_pv, o.at())
                    if ot.n > 1:
                        act.wait_ge(s_ot, ot.at(1))
                    ot.step()
                    act.activation(OS[g % 2][:], PS[:, 4, :], ACT.Copy).then_inc(s_os, 1)

                def widen_reciprocals():
                    rd.step()
                    act.wait_ge(s_rd, rd.at())
                    if dv.n > 0:
                        act.wait_ge(s_ot, dv.at(0))
                    dv.step()
                    act.activation(RDX[:, 0:TPQ * P].rearrange("p (a w) -> p a w", w=pw),
                                   RD[:, 0:TPQ * hpg].unsqueeze(2).to_broadcast([P, TPQ * hpg, pw]),
                                   ACT.Copy).then_inc(s_rx, 1)

                def iteration(first):
                    for g in range(NG):
                        for k in range(NK):
                            exps(k)
                            if k == 0 and not (first and g == 0):
                                copy_sums((g - 1) % NG)
                            if k == 3 and not (first and g == 0):
                                widen_reciprocals()

                iteration(True)
                with act.Fori(1, NQ - 1) as it:
                    n = NG * NK * npair
                    for c, per in ((sc, n), (pv, n), (o, n), (ot, NG), (rd, NG), (dv, NG)):
                        c.loop(it, 1, per)
                    iteration(False)
                    for c in (sc, pv, o, ot, rd, dv):
                        c.end(NQ - 2)
                iteration(False)
                copy_sums(NG - 1)
                widen_reciprocals()
                fence(act, fences)

                f = FFN[L]
                E, ft = f["E"], f["ft"]
                normalize()
                lc.step()
                act.wait_ge(s_lc, lc.at())
                act.activation(PB[:, :, 0:E], LG[:, :, 0:E], ACT.Sigmoid if L == 0 else ACT.Exp).then_inc(s_ex, 1)
                if L in (1, 2):
                    for c in range(NQ):
                        ctc.step()
                        act.wait_ge(s_ct, ctc.at())
                        act.activation(combT[:, c * Q:(c + 1) * Q], PS[0:8, c % 2, :], ACT.Copy).then_inc(s_ctc, 1)
                if L == 2:
                    dn.step(4 * NT)
                else:
                    job = [0]

                    def expert(par):
                        for c in range(NQ):
                            for t, rows in enumerate(ft):
                                h.step()
                                act.wait_ge(s_h, h.at())
                                if f["gated"]:
                                    if hr.n > 1:
                                        act.wait_ge(s_hr, hr.at(1))
                                    hr.step()
                                    act.activation(SG[job[0] % 2][0:rows, :], PS[0:rows, 2 * (job[0] % 2), :],
                                                   ACT.Silu).then_inc(s_sg, 1)
                                else:
                                    if t == 0:
                                        if dn.n > TPQ:
                                            act.wait_ge(s_y, dn.at(TPQ))
                                        dn.step(TPQ)
                                    if L == 0:
                                        act.activation(HT[c % 2][:, t, :], PS[:, job[0] % 4, :],
                                                       ACT.Silu).then_inc(s_hr, 1)
                                    else:
                                        act.activation(HT[c % 2][:, t, :], PS[:, job[0] % 4, :], ACT.Gelu,
                                                       bias=B1[par][:, t:t + 1], scale=1.0).then_inc(s_hr, 1)
                                job[0] += 1

                    if L == 3:
                        expert(0)
                        dn.step(NT)
                    EA = f["EA"]
                    if L < 3:
                        loops = ((h, 2 * NQ * len(ft)), (dn, 2 * NT))
                        with act.Fori(0, EA // 2) as i:
                            for c, per in loops:
                                c.loop(i, 0, per)
                            expert(0)
                            expert(1)
                            for c, per in loops:
                                c.end(EA // 2)
                        hr.step(EA * NQ * len(ft))
                    else:
                        def routed(par):
                            tr.step()
                            act.wait_ge(s_tr, tr.at())
                            act.activation(XT[par][:], PS[:, 6:8, 0:CAP], ACT.Copy).then_inc(s_te, 1)
                            for t, rows in enumerate(ft):
                                h.step()
                                act.wait_ge(s_h, h.at())
                                act.wait_ge(s_hr, hr.at(1))
                                hr.step()
                                act.activation(SG[job[0] % 2][0:rows, 0:CAP],
                                               PS[0:rows, 2 * (job[0] % 2), 0:CAP], ACT.Silu).then_inc(s_sg, 1)
                                job[0] += 1

                        loops = ((h, 2 * len(ft)), (hr, 2 * len(ft)), (tr, 2))
                        with act.Fori(0, 8) as i:
                            for c, per in loops:
                                c.loop(i, 0, per)
                            routed(0)
                            routed(1)
                            for c, per in loops:
                                c.end(8)
                fence(act, fences)

        @block.vector
        def _(dve):
            fences = [0]
            v = Count(s_v)
            std, xt, xtc = Count(s_std), Count(s_xt), Count(s_xtc)
            pc, pd = Count(s_pc), [Count(s) for s in s_pd]
            sj, md = Count(s_sj), Count(s_md)
            os_ = Count(s_os)
            lg, ex = Count(s_lg), Count(s_ex)
            gl = Count(s_gl)
            by = Count(s_by)
            h, sg, dn, y, yf = Count(s_h), Count(s_sg), Count(s_y, Y_FREE), Count(s_y, Y_FREE), Count(s_yf, YF_FREE)
            sf, rx = Count(s_sf), Count(s_rx)
            yd = [Count(q) for q in s_yd]

            def link(ins):
                ins.then_inc(s_v, 1)
                v.step()
                dve.wait_ge(s_v, v.at())

            dve.wait_ge(s_in, 6 * 16)
            link(dve.memset(mask_col[:], 0.0))
            for r, lo, hi in ((P, 0, NK - 1), (KREM, NK - 1, NK)):
                link(dve.tensor_copy(mask_col[0:r, lo:hi], mask_u8[0:r, lo:hi]))
                link(dve.tensor_scalar(mask_col[0:r, lo:hi], mask_col[0:r, lo:hi], 1.0, -MASKED,
                                       ALU.subtract, ALU.mult))
            link(dve.tensor_scalar(mask_row[:], mask_row_u8[:], 1.0, -MASKED, ALU.subtract, ALU.mult))
            fence(dve, fences)

            def normalize(keep=False):
                for t in range(NT):
                    last = dve.bn_stats(stat[:, t, :], X[:, t, :])
                link(last)
                for t in range(NT):
                    last = dve.bn_aggr(mv[:, t, :], stat[:, t, :])
                link(last)
                dve.tensor_scalar(mv[:, :, 1], mv[:, :, 1], EPS, None, ALU.add).then_inc(s_stat, 1)
                std.step()
                dve.wait_ge(s_std, std.at())
                link(dve.reciprocal(rstd[:], rstd[:]))
                for c in range(NQ):
                    if c >= 1:
                        dve.wait_ge(s_xt, xt.at())
                    for i in range(TPQ):
                        t = c * TPQ + i
                        last = dve.tensor_scalar(XN[:, t, :], X[:, t, :], mv[:, t, 0:1], rstd[:, t:t + 1],
                                                 ALU.subtract, ALU.mult)
                    last.then_inc(s_xn, 1)
                    xt.step()
                    dve.wait_ge(s_xt, xt.at())
                    dve.tensor_copy(xnT[:, 0, c * Q:(c + 1) * Q], PS[:, 0, :]).then_inc(s_xtc, 1)
                    if keep:
                        tiles = X[:, c * TPQ:(c + 1) * TPQ, :]
                        link(dve.tensor_tensor(tiles, tiles, XN[:, c * TPQ:(c + 1) * TPQ, :], ALU.add))
                fence(dve, fences)

            for L in range(4):
                a = ATT[L]
                dh, pw, hpg, nsub = a["dh"], a["pw"], a["hpg"], a["nsub"]
                units = hpg * TPQ
                scale = 0.25 if dh == 16 else 32.0 ** -0.5
                normalize()

                for u in range(16):
                    kind, c = u // 8, u % 4
                    n = Q if kind == 0 else min(Q, S - c * Q)
                    x, r, p = QK[u % 2][:, 0:n], QR[u % 2][:, 0:n], QP[u % 2]
                    pc.step()
                    dve.wait_ge(s_pc, pc.at())
                    if kind == 0:
                        link(dve.tensor_scalar(x, x, scale, None, ALU.mult))
                    if pd[u % 2].n > 0:
                        dve.wait_ge(s_pd[u % 2], pd[u % 2].at())
                    pd[u % 2].step(16)
                    link(dve.tensor_copy(p[:, 0, 0:n], x))
                    link(dve.tensor_tensor(r, x, p[:, 0, 0:n], ALU.subtract))
                    link(dve.tensor_copy(p[:, 1, 0:n], r))
                    dve.tensor_tensor(p[:, 2, 0:n], r, p[:, 1, 0:n], ALU.subtract).then_inc(s_pp, 1)
                fence(dve, fences)

                njob = [0]

                nd = TPQ * hpg

                def side(job, it):
                    bank = 5 + njob[0] % 3
                    njob[0] += 1
                    sj.step()
                    if job[0] == "turn":
                        if md.n > 0:
                            dve.wait_ge(s_md, md.at())
                        md.step(16)
                    dve.wait_ge(s_sj, sj.at())
                    if job[0] == "max":
                        _, g, u, c = job
                        ins = dve.reduce_max(MX4[g % 2][:, u, c:c + 1], PS[:, bank, 0:CK[c]], AX.X)
                        ins.then_inc(s_sf, 1)
                        if u == units - 1 and c == 3:
                            dve.wait_ge(s_sf, sf.at())
                            dve.reduce_max(MX[g % 2][:, 0:units], MX4[g % 2][:, 0:units, :], AX.X).then_inc(s_mx, 1)
                    elif job[0] == "turn":
                        neg, rest = MN[0:units, :], MR[0:units, :]
                        dve.tensor_scalar(neg, PS[0:units, bank, 0:P], -1.0, None, ALU.mult).then_inc(s_sf, 1)
                        dve.wait_ge(s_sf, sf.at())
                        link(dve.tensor_copy(MP[0:units, 1, :], neg))
                        link(dve.tensor_tensor(rest, neg, MP[0:units, 1, :], ALU.subtract))
                        link(dve.tensor_copy(MP[0:units, 2, :], rest))
                        dve.tensor_tensor(MP[0:units, 3, :], rest, MP[0:units, 2, :], ALU.subtract).then_inc(s_mp, 1)
                    elif job[0] == "den":
                        g = job[1]
                        if rx.n > 0:
                            dve.wait_ge(s_rx, rx.at(0))
                        rx.step()
                        dve.reciprocal(RD[:, 0:nd], PS[:, bank, 0:nd]).then_inc(s_sf, 1)
                        dve.wait_ge(s_sf, sf.at())
                        dve.sem_inc(s_rd, 1)
                    elif job[0] == "spread":
                        g = job[1]
                        dve.tensor_tensor(OT[:, g, :], OS[g % 2][:], PS[:, bank, :], ALU.mult).then_inc(s_sf, 1)
                        dve.wait_ge(s_sf, sf.at())
                        dve.sem_inc(s_ot, 1)
                    else:
                        t = (it - 1) * TPQ + job[1]
                        x = X[:, bass.ds(t, 1), :].rearrange("p a d -> p (a d)") if not isinstance(t, int) else X[:, t, :]
                        dve.tensor_tensor(x, x, PS[:, bank, 0:D], ALU.add).then_inc(s_sf, 1)

                def sides(jobs, it):
                    for job in jobs:
                        sf.step()
                        side(job, it)

                sides(side_prologue(hpg), 0)

                def iteration(it, first, last):
                    njob[0] = 0
                    for g in range(NG):
                        for slot in side_schedule(g, hpg, first, last):
                            sides(slot, it)

                per = sum(len(s) for g in range(NG) for s in side_schedule(g, hpg, False, False))
                iteration(0, True, False)
                with dve.Fori(1, NQ - 1) as it:
                    loops = ((sj, per), (sf, per), (md, 64), (v, 4 * 3), (rx, NG))
                    for c, p in loops:
                        c.loop(it, 1, p)
                    iteration(it, False, False)
                    for c, p in loops:
                        c.end(NQ - 2)
                iteration(NQ - 1, False, True)
                njob[0] = 0
                sides([("den", NG - 1), ("spread", NG - 1)] + [("out", i) for i in range(TPQ)], NQ)
                fence(dve, fences)

                f = FFN[L]
                E, ft, topk = f["E"], f["ft"], f["topk"]
                normalize(keep=L == 3)
                nl = {0: 16, 1: 32, 2: 48, 3: 32}[L]
                gl.step(nl)
                lg.step()
                dve.wait_ge(s_lg, lg.at())
                l, pb, sl, mk, rk = (z[:, :, 0:E] for z in (LG, PB, SL, MK, RK))

                def wide(z, n=E):
                    return z[:].unsqueeze(2).to_broadcast([P, NT, n])

                def rank(z, out_, n):
                    for t in range(0, NT, 4):
                        zi = z[:, t:t + 4, :].unsqueeze(3).to_broadcast([P, 4, n, n])
                        zj = z[:, t:t + 4, :].unsqueeze(2).to_broadcast([P, 4, n, n])
                        gt, eq = BIG[0][:, :, 0:n, 0:n], BIG[1][:, :, 0:n, 0:n]
                        link(dve.tensor_tensor(gt, zj, zi, ALU.is_gt))
                        link(dve.tensor_tensor(eq, zj, zi, ALU.is_equal))
                        for i in range(4):
                            last = dve.tensor_tensor(eq[:, i], eq[:, i], less[:, 0:n, 0:n], ALU.mult)
                        link(last)
                        for i in range(4):
                            last = dve.tensor_tensor(gt[:, i], gt[:, i], eq[:, i], ALU.add)
                        link(last)
                        link(dve.tensor_reduce(out_[:, t:t + 4, :], gt, AX.X, ALU.add))

                dve.wait_ge(s_gl, gl.at())
                if L >= 2:
                    gb = GB[:, 0:E].unsqueeze(1).to_broadcast([P, NT, E])
                    link(dve.tensor_tensor(l, PS[:, 0, 0:NT * E].rearrange("p (t e) -> p t e", e=E), gb, ALU.add))
                else:
                    link(dve.tensor_copy(l, PS[:, 0, 0:NT * E].rearrange("p (t e) -> p t e", e=E)))
                if L > 0:
                    link(dve.reduce_max(R1[:], l, AX.X))
                    if L == 1:
                        rank(l, rk, E)
                    dve.tensor_tensor(l, l, wide(R1), ALU.subtract).then_inc(s_lc, 1)
                else:
                    dve.memset(R1[:], 0.0).then_inc(s_lc, 1)
                ex.step()
                dve.wait_ge(s_ex, ex.at())
                if L == 0:
                    p4 = PB[:].rearrange("p t (g i) -> p t g i", i=4)
                    s0, s1, s2, s3 = (p4[:, :, :, i] for i in range(4))
                    hi0, lo0, hi1, lo1, best, sec = (z[:] for z in T4)
                    link(dve.tensor_tensor(hi0, s0, s1, ALU.max))
                    link(dve.tensor_tensor(lo0, s0, s1, ALU.min))
                    link(dve.tensor_tensor(hi1, s2, s3, ALU.max))
                    link(dve.tensor_tensor(lo1, s2, s3, ALU.min))
                    link(dve.tensor_tensor(best, hi0, hi1, ALU.max))
                    link(dve.tensor_tensor(sec, hi0, hi1, ALU.min))
                    link(dve.tensor_tensor(lo0, lo0, lo1, ALU.max))
                    link(dve.tensor_tensor(sec, sec, lo0, ALU.max))
                    link(dve.tensor_tensor(best, best, sec, ALU.add))
                    rank(T4[4][:], T4[0][:], 4)
                    link(dve.tensor_scalar(T4[0][:], T4[0][:], 2.0, None, ALU.is_lt))
                    m4 = MK[:].rearrange("p t (g i) -> p t g i", i=4)
                    for i in range(4):
                        last = dve.tensor_tensor(m4[:, :, :, i], p4[:, :, :, i], T4[0][:], ALU.mult)
                    link(last)
                    rank(mk, rk, E)
                elif L >= 2:
                    link(dve.tensor_reduce(R1[:], pb, AX.X, ALU.add))
                    link(dve.reciprocal(R1[:], R1[:]))
                    link(dve.tensor_tensor(pb, pb, wide(R1), ALU.mult))
                    rank(pb, rk, E)
                link(dve.tensor_scalar(sl, rk, float(topk), None, ALU.is_lt))
                link(dve.tensor_tensor(pb, pb, sl, ALU.mult))
                link(dve.tensor_reduce(R1[:], pb, AX.X, ALU.add))
                if L in (0, 3):
                    link(dve.tensor_scalar(R1[:], R1[:], 1e-20 if L == 0 else 1e-9, None, ALU.add))
                link(dve.reciprocal(R1[:], R1[:]))
                if L == 0:
                    link(dve.tensor_scalar(R1[:], R1[:], 2.5, None, ALU.mult))
                cb = comb[:, :, 0:E]
                if L < 3:
                    dve.tensor_tensor(cb, pb, wide(R1), ALU.mult).then_inc(s_cb, 1)
                else:
                    link(dve.tensor_tensor(pb, pb, wide(R1), ALU.mult))
                    dve.memset(TOT[:, 0, :], 0.0).then_inc(s_cb, 1)
                    by.step()
                    dve.wait_ge(s_by, by.at())
                    dve.wait_ge(s_cb, 4)
                    for t in range(NT - 1):
                        link(dve.tensor_tensor(TOT[:, t + 1, :], TOT[:, t, :], PS[:, 2, 16 * t:16 * t + 16], ALU.add))
                    link(dve.tensor_tensor(POS[:], TOT[:, 0:NT, :], PS[:, 1, 0:256].rearrange("p (t e) -> p t e", e=16), ALU.add))
                    link(dve.tensor_scalar(WI[:], POS[:], float(CAP), None, ALU.is_lt))
                    link(dve.tensor_tensor(cb, pb, WI[:], ALU.mult))
                    link(dve.tensor_tensor(POS[:], POS[:], first_place[:].unsqueeze(1).to_broadcast([P, NT, 16]), ALU.add))
                    link(dve.tensor_scalar(WI[:], WI[:], -1.0, -float(PLACES), ALU.add, ALU.mult))
                    link(dve.tensor_tensor(POS[:], POS[:], WI[:], ALU.add))
                    for r in range(2):
                        link(dve.tensor_scalar(WI[:], rk, float(r), None, ALU.is_equal))
                        link(dve.tensor_tensor(MK[:], WI[:], POS[:], ALU.mult))
                        link(dve.tensor_reduce(IP[r][:], MK[:], AX.X, ALU.add))
                        link(dve.tensor_copy(IS[r][:], IP[r][:]))
                        link(dve.tensor_scalar(IP[r][:], IP[r][:], float(PLACES - 1), None, ALU.min))
                        link(dve.tensor_copy(IG[r][:], IP[r][:]))
                        link(dve.tensor_tensor(MK[:], WI[:], cb, ALU.mult))
                        link(dve.tensor_reduce(WR[r][:], MK[:], AX.X, ALU.add))
                    dve.sem_inc(s_cb, 1)
                    dve.sem_inc(s_ix, 1)
                if L in (1, 2):
                    for t in range(NT):
                        by.step()
                        dve.wait_ge(s_by, by.at())
                        dve.tensor_tensor(X[:, t, :], X[:, t, :], PS[:, 4 + t % 4, 0:D], ALU.add).then_inc(s_yf, 1)
                        yf.step()

                def add_tile(t, e):
                    y.step()
                    dve.wait_ge(s_y, y.at())
                    if yf.n > 3:
                        dve.wait_ge(s_yf, yf.at(3))
                    yf.step()
                    b = 4 + nyt[0] % 4
                    nyt[0] += 1
                    if isinstance(e, int):
                        c = comb[:, t, e:e + 1]
                    else:
                        c = comb[:, t, bass.ds(e, 1)]
                    dve.scalar_tensor_tensor(X[:, t, :], PS[:, b, 0:D], c, X[:, t, :], ALU.mult, ALU.add).then_inc(s_yf, 1)

                nyt = [0]
                hjob = [0]

                def expert(e):
                    for c in range(NQ + 1):
                        if c < NQ and f["gated"]:
                            for t, rows in enumerate(ft):
                                sg.step()
                                dve.wait_ge(s_sg, sg.at())
                                h.step()
                                dve.wait_ge(s_h, h.at())
                                if t == 0:
                                    if dn.n > TPQ:
                                        dve.wait_ge(s_y, dn.at(TPQ))
                                    dn.step(TPQ)
                                p = hjob[0] % 2
                                hjob[0] += 1
                                dve.tensor_tensor(HT[c % 2][0:rows, t, :], SG[p][0:rows, :],
                                                  PS[0:rows, 2 * p + 1, :], ALU.mult).then_inc(s_hr, 1)
                        if c >= 1:
                            for i in range(TPQ):
                                add_tile((c - 1) * TPQ + i, e)

                if L == 2:
                    dn.step(4 * NT)
                    with dve.Fori(0, 2) as i:
                        y.loop(i, 0, 32)
                        yf.loop(i, 0, 64)
                        for par in range(2):
                            for t in range(NT):
                                y.step()
                                dve.wait_ge(s_y, y.at())
                                for k in range(2):
                                    dve.wait_ge(s_yf, yf.at())
                                    yf.step()
                                    dve.scalar_tensor_tensor(
                                        X[:, t, :], PS[:, t % 8, k * D:(k + 1) * D],
                                        comb[:, t, bass.ds(i * 4 + par * 2 + k, 1)], X[:, t, :],
                                        ALU.mult, ALU.add).then_inc(s_yf, 1)
                        y.end(2)
                        yf.end(2)
                else:
                    EA = f["EA"]
                    if L < 3:
                        with dve.Fori(0, EA // 2) as i:
                            loops = [(y, 2 * NT), (yf, 2 * NT)]
                            for c, p in loops:
                                c.loop(i, 0, p)
                            expert(i * 2)
                            expert(i * 2 + 1)
                            for c, p in loops:
                                c.end(EA // 2)
                        h.step(EA * NQ * len(ft))
                        dn.step(EA * NT)
                    else:
                        expert(16)

                        def answers(par):
                            if yd[par].n > 0:
                                dve.wait_ge(s_yd[par], yd[par].at())
                            yd[par].step(32)
                            for t in range(CT):
                                r = P if t < CT - 1 else CLAST
                                y.step()
                                dve.wait_ge(s_y, y.at())
                                dve.tensor_copy(YE[par][0:r, t, :], PS[0:r, 4 + t % 2, 0:D]).then_inc(s_yc, 1)

                        def products(par):
                            for t, rows in enumerate(ft):
                                sg.step()
                                dve.wait_ge(s_sg, sg.at())
                                h.step()
                                dve.wait_ge(s_h, h.at())
                                p = hjob[0] % 2
                                hjob[0] += 1
                                dve.tensor_tensor(HT[par][0:rows, t, 0:CAP], SG[p][0:rows, 0:CAP],
                                                  PS[0:rows, 2 * p + 1, 0:CAP], ALU.mult).then_inc(s_hr, 1)

                        products(0)
                        answers(0)
                        products(1)
                        with dve.Fori(1, 8) as i:
                            loops = [(y, 2 * CT), (sg, 2 * len(ft)), (h, 2 * len(ft)), (yd[0], 32), (yd[1], 32)]
                            for c, p in loops:
                                c.loop(i, 1, p)
                            for par in range(2):
                                answers(1 - par)
                                products(par)
                            for c, p in loops:
                                c.end(7)
                        answers(1)
                        for t in range(NT):
                            for r in range(2):
                                k = 2 * t + r
                                dve.wait_ge(s_yg[k % 4], 16 * (k // 4 + 1))
                                if r == 1:
                                    dve.wait_ge(s_ix, 1 + k)
                                dve.scalar_tensor_tensor(X[:, t, :], YG[k % 4][:], WR[r][:, t:t + 1], X[:, t, :],
                                                         ALU.mult, ALU.add).then_inc(s_ix, 1)
                fence(dve, fences)

        @block.tensor
        def _(pe):
            fences = [0]
            mm = pe.matmul
            xn, xtc, wa = Count(s_xn), Count(s_xtc), Count(s_wa)
            pc, vc = Count(s_pc), Count(s_vc)
            ks, ql, mr = Count(s_ks), [Count(s) for s in s_ql], Count(s_mr)
            pr, use, cs, rx, os_, ot, sf, mx = Count(s_pr), Count(s_pr), Count(s_os), Count(s_rx), Count(s_os), Count(s_ot), Count(s_sf), Count(s_mx)
            gl, cb, ctc, yf = Count(s_gl), Count(s_cb), Count(s_ctc), Count(s_yf, YF_FREE)
            w, hr = [Count(s) for s in s_w], Count(s_hr, HR_FREE)
            xe, te, yc = [Count(q) for q in s_xe], Count(s_te), Count(s_yc)
            fence(pe, fences)

            def normalize():
                for c in range(NQ):
                    xn.step()
                    pe.wait_ge(s_xn, xn.at())
                    if xtc.n > 0:
                        pe.wait_ge(s_xtc, xtc.at())
                    xtc.step(2)
                    for half in range(2):
                        for i in range(TPQ):
                            last = pe.transpose(PS[:, half, i * P:(i + 1) * P],
                                                XN[:, c * TPQ + i, half * P:(half + 1) * P], ident[:])
                    last.then_inc(s_xt, 1)
                fence(pe, fences)

            for L in range(4):
                a = ATT[L]
                dh, pw, hpg, nsub = a["dh"], a["pw"], a["hpg"], a["nsub"]
                npair, units = hpg // 2, hpg * TPQ
                normalize()

                wa.step(16 * (9 + hpg if L < 3 else 5 + hpg))
                pe.wait_ge(s_wa, wa.at())
                for u in range(16):
                    kind, m, c = u // 8, (u // 4) % 2, u % 4
                    n = Q if kind == 0 else min(Q, S - c * Q)
                    if pc.n > 3:
                        pe.wait_ge(s_pc, pc.at(3))
                    pc.step()
                    o, cols = PS[:, u % 4, 0:n], slice(m * P, (m + 1) * P)
                    if kind == 0:
                        mm(o, WQ[:, 0, cols], xnT[:, 0, c * Q:c * Q + n], start=True, stop=False)
                        mm(o, WQ[:, 1, cols], xnT[:, 1, c * Q:c * Q + n], start=False, stop=True).then_inc(s_pj, 1)
                    else:
                        mm(o, WK0[:, cols], C0[:, c * Q:c * Q + n], start=True, stop=False)
                        mm(o, WK1[:, cols], C1[:, c * Q:c * Q + n], start=False, stop=True).then_inc(s_pj, 1)
                    if u < NK:
                        if vc.n > 3:
                            pe.wait_ge(s_vc, vc.at(3))
                        vc.step()
                        r = key_rows(u)
                        o, ks_ = PS[0:r, 4 + u % 4, :], slice(u * P, u * P + r)
                        mm(o, C0[:, ks_], WV0[:], start=True, stop=False)
                        mm(o, C1[:, ks_], WV1[:], start=False, stop=True).then_inc(s_vj, 1)
                fence(pe, fences)

                ks.step(16 * (6 + (16 if L == 3 else 0)))
                pe.wait_ge(s_ks, ks.at())
                for q in range(3):
                    ql[q].step(7 * 16)
                njob, pair, used = [0], [0], [0]
                sel = sel16 if dh == 16 else sel32

                def slot_of(j):
                    return j * nsub

                def side(job):
                    bank = 5 + njob[0] % 3
                    fresh = njob[0] < 3
                    njob[0] += 1
                    if job[0] == "max":
                        _, g, u, c = job
                        if u == 0 and c == 0:
                            pe.wait_ge(s_ql[g], ql[g].at())
                    elif job[0] == "turn":
                        mx.step()
                        pe.wait_ge(s_mx, mx.at())
                    elif job[0] == "den":
                        os_.step()
                        pe.wait_ge(s_os, os_.at())
                    elif job[0] == "spread":
                        rx.step()
                        pe.wait_ge(s_rx, rx.at())
                    elif job[1] == 0:
                        if ot.n > 0:
                            pe.wait_ge(s_ot, ot.at())
                    if njob[0] == 1:
                        if sf.n > 0:
                            pe.wait_ge(s_sf, sf.at(0))
                    elif not fresh:
                        if sf.n > 2:
                            pe.wait_ge(s_sf, sf.at(2))
                    sf.step()
                    if job[0] == "max":
                        _, g, u, c = job
                        j, qt = u // TPQ, u % TPQ
                        for sub in range(nsub):
                            rows = 97 if sub == 0 else 96
                            s = slot_of(j) + sub
                            ks0 = (g * hpg + j) * nsub + sub
                            last = mm(PS[:, bank, 0:CK[c]], QS[g][0:rows, s, qt * P:(qt + 1) * P],
                                      KS[0:rows, ks0, CKO[c]:CKO[c] + CK[c]], start=sub == 0, stop=sub == nsub - 1)
                    elif job[0] == "turn":
                        last = pe.transpose(PS[0:units, bank, 0:P], MX[job[1] % 2][:, 0:units], ident[:])
                    elif job[0] == "den":
                        for i in range(TPQ):
                            last = mm(PS[:, bank, i * hpg:(i + 1) * hpg], OS[job[1] % 2][:, i * P:(i + 1) * P],
                                      sel[:, 0:hpg], start=True, stop=True)
                    elif job[0] == "spread":
                        for i in range(TPQ):
                            last = pe.transpose(PS[:, bank, i * P:(i + 1) * P], RDX[:, i * P:(i + 1) * P], ident[:])
                        ot.step()
                    else:
                        i = job[1]
                        for g in range(NG):
                            last = mm(PS[:, bank, 0:D], OT[:, g, i * P:(i + 1) * P], WO[:, g, :],
                                      start=g == 0, stop=g == NG - 1)
                    last.then_inc(s_sj, 1)

                def scores(g, k, j, i):
                    r = key_rows(k)
                    b = 2 * (pair[0] % 2)
                    if i == 0:
                        if pr.n > 1:
                            pe.wait_ge(s_pr, pr.at(1))
                        pr.step()
                    jj = 2 * j + i
                    for sub in range(nsub):
                        rows = 100 if sub == 0 else 96
                        last = mm(PS[0:r, b + i, :], KS[0:rows, (g * hpg + jj) * nsub + sub, k * P:k * P + r],
                                  QS[g][0:rows, slot_of(jj) + sub, :], start=sub == 0, stop=sub == nsub - 1)
                    if i == 1:
                        pair[0] += 1
                        last.then_inc(s_sc, 1)

                def weigh(g, k):
                    r = key_rows(k)
                    for j in range(npair):
                        use.step()
                        pe.wait_ge(s_pr, use.at())
                        for i in range(2):
                            jj = 2 * j + i
                            last = mm(PS[pw * jj:pw * jj + pw, 4, :],
                                      V[0:r, k, (g * hpg + jj) * pw:(g * hpg + jj) * pw + pw],
                                      PR[used[0] % 4][0:r, i, :], start=k == 0, stop=k == NK - 1,
                                      skip_group_check=True)
                        used[0] += 1
                        last.then_inc(s_pv, 1)

                for job in side_prologue(hpg):
                    side(job)

                def iteration(first, last):
                    njob[0] = 0
                    for g in range(NG):
                        if not (last and g > 0):
                            ql[(g + 3) % 4].step(7 * 16)
                        mr.step(16)
                        pe.wait_ge(s_mr, mr.at())
                        for k, slot in enumerate(side_schedule(g, hpg, first, last)):
                            for job in slot[:2]:
                                side(job)
                            cut = [2 + n for n in chunk_of(max(len(slot) - 2, 0), 2 * npair)]
                            for j in range(npair):
                                for i in range(2):
                                    scores(g, k, j, i)
                                    for job in slot[cut[2 * j + i]:cut[2 * j + i + 1]]:
                                        side(job)
                            if k == 0 and not (first and g == 0):
                                weigh((g - 1) % NG, NK - 1)
                            elif k > 0:
                                if k == 1 and not (first and g == 0):
                                    cs.step()
                                    pe.wait_ge(s_os, cs.at())
                                weigh(g, k - 1)

                njobs = sum(len(s) for g in range(NG) for s in side_schedule(g, hpg, False, False))
                iteration(True, False)
                with pe.Fori(1, NQ - 1) as it:
                    loops = [(mr, 64), (pr, NG * NK * npair), (use, NG * NK * npair), (cs, NG), (os_, NG), (ot, NG), (rx, NG),
                             (sf, njobs), (mx, NG)] + [(c, 7 * 16) for c in ql]
                    for c, p in loops:
                        c.loop(it, 1, p)
                    iteration(False, False)
                    for c, p in loops:
                        c.end(NQ - 2)
                iteration(False, True)
                weigh(NG - 1, NK - 1)
                njob[0] = 0
                for job in [("den", NG - 1), ("spread", NG - 1)] + [("out", i) for i in range(TPQ)]:
                    side(job)
                cs.step()
                fence(pe, fences)

                f = FFN[L]
                E, ft = f["E"], f["ft"]
                normalize()
                gl.step({0: 16, 1: 32, 2: 48, 3: 32}[L])
                pe.wait_ge(s_gl, gl.at())
                for t in range(NT):
                    for k in range(2):
                        last = mm(PS[:, 0, t * E:(t + 1) * E], xnT[:, k, t * P:(t + 1) * P], GW[:, k, 0:E],
                                  start=k == 0, stop=k == 1)
                last.then_inc(s_lg, 1)
                cb.step()
                pe.wait_ge(s_cb, cb.at())
                if L == 3:
                    sl = SL[:].rearrange("p t e -> p (t e)")
                    mm(PS[:, 1, 0:256], tri[:], sl, start=True, stop=True)
                    mm(PS[:, 2, 0:256], ones[:], sl, start=True, stop=True).then_inc(s_by, 1)
                    cb.step()
                    pe.wait_ge(s_cb, cb.at())
                if L in (1, 2):
                    for c in range(NQ):
                        if ctc.n > 1:
                            pe.wait_ge(s_ctc, ctc.at(1))
                        ctc.step()
                        for i in range(TPQ):
                            last = pe.transpose(PS[0:8, c % 2, i * P:(i + 1) * P], comb[:, c * TPQ + i, 0:8], ident[:])
                        last.then_inc(s_ct, 1)
                    pe.wait_ge(s_ctc, ctc.at())
                    for t in range(NT):
                        if yf.n > 3:
                            pe.wait_ge(s_yf, yf.at(3))
                        yf.step()
                        mm(PS[:, 4 + t % 4, 0:D], combT[:, t * P:(t + 1) * P], B2[:], start=True, stop=True).then_inc(s_by, 1)

                hj, yj = [0], [0]

                def expert(par):
                    F = sum(ft)
                    W = 2 * F if f["gated"] else F
                    w[par].step({0: 32, 1: 48, 3: 48}[L])
                    pe.wait_ge(s_w[par], w[par].at())
                    up = WU[par][:, 0:2 * W].rearrange("p (k f) -> p k f", k=2)
                    for c in range(NQ + 1):
                        if c < NQ:
                            at = 0
                            for t, rows in enumerate(ft):
                                if f["gated"]:
                                    if hr.n > 1:
                                        pe.wait_ge(s_hr, hr.at(1))
                                    banks = [(2 * (hj[0] % 2), 0), (2 * (hj[0] % 2) + 1, F)]
                                else:
                                    if hr.n > 3:
                                        pe.wait_ge(s_hr, hr.at(3))
                                    banks = [(hj[0] % 4, 0)]
                                hr.step()
                                hj[0] += 1
                                for b, off in banks:
                                    for k in range(2):
                                        last = mm(PS[0:rows, b, :], up[:, k, off + at:off + at + rows],
                                                  xnT[:, k, c * Q:(c + 1) * Q], start=k == 0, stop=k == 1)
                                at += rows
                                last.then_inc(s_h, 1)
                        if c >= 1:
                            lag = len(ft) if c < NQ else 0
                            if hr.n > lag:
                                pe.wait_ge(s_hr, hr.at(lag))
                            for i in range(TPQ):
                                if yf.n > 3:
                                    pe.wait_ge(s_yf, yf.at(3))
                                yf.step()
                                b = 4 + yj[0] % 4
                                yj[0] += 1
                                for t, rows in enumerate(ft):
                                    last = mm(PS[:, b, 0:D], HT[(c - 1) % 2][0:rows, t, i * P:(i + 1) * P],
                                              WD[par][0:rows, t, :], start=t == 0, stop=t == len(ft) - 1)
                                last.then_inc(s_y, 1)

                if L == 2:
                    pe.wait_ge(s_yf, yf.at())
                    with pe.Fori(0, 2) as i:
                        loops = [(yf, 64), (w[0], 16), (w[1], 16)]
                        for c, p in loops:
                            c.loop(i, 0, p)
                        for par in range(2):
                            w[par].step(16)
                            pe.wait_ge(s_w[par], w[par].at())
                            for t in range(NT):
                                if yf.n > 14:
                                    pe.wait_ge(s_yf, yf.at(14))
                                yf.step(2)
                                for k in range(2):
                                    last = mm(PS[:, t % 8, :], xnT[:, k, t * P:(t + 1) * P],
                                              WU[par][:, k * 512:(k + 1) * 512], start=k == 0, stop=k == 1)
                                last.then_inc(s_y, 1)
                        for c, p in loops:
                            c.end(2)
                else:
                    EA = f["EA"]
                    nw = {0: 32, 1: 48, 3: 48}[L]
                    if L < 3:
                        with pe.Fori(0, EA // 2) as i:
                            loops = [(hr, 2 * NQ * len(ft)), (yf, 2 * NT), (w[0], nw), (w[1], nw)]
                            for c, p in loops:
                                c.loop(i, 0, p)
                            expert(0)
                            expert(1)
                            for c, p in loops:
                                c.end(EA // 2)
                    else:
                        expert(0)
                        pe.wait_ge(s_yf, yf.at())

                        def rows_in(par):
                            xe[par].step(32)
                            pe.wait_ge(s_xe[par], xe[par].at())
                            if te.n > 0:
                                pe.wait_ge(s_te, te.at())
                            te.step()
                            for half in range(2):
                                for t in range(CT):
                                    r = P if t < CT - 1 else CLAST
                                    last = pe.transpose(PS[:, 6 + half, t * P:t * P + r],
                                                        XE[par][0:r, t, half * P:(half + 1) * P], ident[0:r, 0:r])
                            last.then_inc(s_tr, 1)

                        def hidden(par):
                            F = sum(ft)
                            w[1 - par].step(nw)
                            pe.wait_ge(s_w[1 - par], w[1 - par].at())
                            pe.wait_ge(s_te, te.at())
                            up = WU[1 - par][:, 0:4 * F].rearrange("p (k f) -> p k f", k=2)
                            at = 0
                            for t, rows in enumerate(ft):
                                pe.wait_ge(s_hr, hr.at(1))
                                hr.step()
                                b = 2 * (hj[0] % 2)
                                hj[0] += 1
                                for v in range(2):
                                    for k in range(2):
                                        last = mm(PS[0:rows, b + v, 0:CAP], up[:, k, v * F + at:v * F + at + rows],
                                                  XT[par][:, k, :], start=k == 0, stop=k == 1)
                                at += rows
                                last.then_inc(s_h, 1)

                        def answer(par):
                            pe.wait_ge(s_hr, hr.at())
                            for t in range(CT):
                                r = P if t < CT - 1 else CLAST
                                if yc.n > 1:
                                    pe.wait_ge(s_yc, yc.at(1 if t else 0))
                                yc.step()
                                for q, rows in enumerate(ft):
                                    last = mm(PS[0:r, 4 + t % 2, 0:D], HT[par][0:rows, q, t * P:t * P + r],
                                              WD[1 - par][0:rows, q, :], start=q == 0, stop=q == len(ft) - 1)
                                last.then_inc(s_y, 1)

                        rows_in(0)
                        hidden(0)
                        rows_in(1)
                        answer(0)
                        hidden(1)
                        with pe.Fori(1, 8) as i:
                            loops = [(hr, 2 * len(ft)), (w[0], nw), (w[1], nw), (xe[0], 32), (xe[1], 32),
                                     (te, 2), (yc, 2 * CT)]
                            for c, p in loops:
                                c.loop(i, 1, p)
                            for par in range(2):
                                rows_in(par)
                                answer(1 - par)
                                hidden(par)
                            for c, p in loops:
                                c.end(7)
                        answer(1)
                fence(pe, fences)


def kernel(x, ctx_768, mask_BxS2_bf1, **w):
    import numpy as np
    import concourse.bacc as bacc
    from concourse.bass_utils import run_bass_kernel_spmd

    w = {k: np.asarray(v) for k, v in w.items()}
    a = {}

    def contraction_first(m, n):
        lead = m.shape[:-2]
        m = m.reshape(*lead, n, P, m.shape[-1])
        return np.moveaxis(m, -3, -2).reshape(*lead, P, n * m.shape[-1])

    a["x"] = np.asarray(x)[0]
    a["ctx_t"] = np.asarray(ctx_768)[0].T
    a["mask"] = np.asarray(mask_BxS2_bf1).view(np.uint8)
    wkv = w["L0_xattn_Wkv"].reshape(16, 2, 16, DC)
    bkv = w["L0_xattn_bkv"].reshape(16, 2, 16)
    a["wq0"], a["bq0"] = w["L0_xattn_Wq"].T, w["L0_xattn_bq"]
    a["wk0"], a["bk0"] = wkv[:, 0].reshape(D, DC).T, bkv[:, 0].reshape(D)
    a["wv0"], a["bv0"] = wkv[:, 1].reshape(D, DC).T, bkv[:, 1].reshape(D)
    a["wo0"], a["bo0"] = w["L0_xattn_Wo"].T, w["L0_xattn_bo"]
    for n in "qkvo":
        a[f"w{n}1"], a[f"b{n}1"] = w[f"L1_xattn_w{n}"], w[f"L1_xattn_b{n}"]
        a[f"w{n}2"], a[f"b{n}2"] = w[f"L2_xattn_W{n}"].T, w[f"L2_xattn_b{n}"]
        a[f"w{n}3"] = w[f"L3_xattn_W{n}"]
    a["gw0"], a["gw1"] = w["L0_ffn_gate_weight"].T, w["L1_ffn_router_w"].T
    a["gw2"], a["gb2"] = w["L2_ffn_Wg"], w["L2_ffn_bg"]
    a["gw3"], a["gb3"] = w["L3_ffn_router_w"], w["L3_ffn_router_b"]
    up = np.concatenate([w["L0_ffn_expert_up"], np.moveaxis(w["L0_ffn_shared_up"].reshape(D, 4, P), 1, 0)])
    a["up0"] = contraction_first(up, 2)
    a["down0"] = np.concatenate([w["L0_ffn_expert_down"], w["L0_ffn_shared_down"].reshape(4, P, D)])
    a["up1"] = contraction_first(np.swapaxes(w["L1_ffn_w1"], 1, 2), 2)
    a["down1"] = contraction_first(np.swapaxes(w["L1_ffn_w2"], 1, 2), 8)
    a["b1"] = np.swapaxes(w["L1_ffn_b1"].reshape(8, 8, P), 1, 2)
    a["b2_1"], a["b2_2"] = w["L1_ffn_b2"], w["L2_ffn_be"]
    we = np.moveaxis(w["L2_ffn_We"].reshape(4, 2, D, D), 3, 1).reshape(4, D, 2 * D)
    a["we2"] = contraction_first(we, 2)
    gate = np.concatenate([w["L3_ffn_w_gate"], w["L3_ffn_sw_gate"][None]])
    upw = np.concatenate([w["L3_ffn_w_up"], w["L3_ffn_sw_up"][None]])
    down = np.concatenate([w["L3_ffn_w_down"], w["L3_ffn_sw_down"][None]])
    a["up3"] = contraction_first(np.concatenate([gate, upw], axis=-1), 2)
    a["down3"] = contraction_first(down[:, 0:2 * P], 2)
    a["down3b"] = down[:, 2 * P:]

    nc = bacc.Bacc("TRN2", target_bir_lowering=False, num_devices=1)
    arrays, aps = {}, {}
    for name, v in a.items():
        v = np.ascontiguousarray(v)
        arrays[f"in_{name}"] = v
        aps[name] = nc.dram_tensor(f"in_{name}", v.shape, mybir.dt.from_np(v.dtype), kind="ExternalInput").ap()
    out = nc.dram_tensor("out_x", (T, D), mybir.dt.float32, kind="ExternalOutput").ap()
    build(nc, aps, out)
    r = run_bass_kernel_spmd(nc, [arrays], core_ids=[0])
    return r.results[0]["out_x"].reshape(1, T, D)
```

```python
import concourse.bass as bass
from concourse import mybir
from contextlib import ExitStack

T, D, S, DC = 2048, 256, 1601, 192
P = 128
NT = T // P
Q = 512
NQ = T // Q
TPQ = Q // P
NK = (S + P - 1) // P
KREM = S - (NK - 1) * P
NG = 4
CK = [401, 400, 400, 400]
CKO = [0, 401, 801, 1201]
MASKED = -float(2.0 ** 127)
CAP = 320
CT = (CAP + P - 1) // P
CLAST = CAP - (CT - 1) * P
TILES = 2 * NT + 7
PLACES = max(16 * CAP, (TILES + 1) * P)
NF = 1024
EARLY = 5
EPS = 1e-5

ATT = [dict(dh=16, pw=32, hpg=4, nsub=1), dict(dh=16, pw=32, hpg=4, nsub=1),
       dict(dh=32, pw=64, hpg=2, nsub=2), dict(dh=16, pw=32, hpg=4, nsub=1)]
FFN = [dict(E=16, EA=20, ft=[128], gated=False, topk=4),
       dict(E=8, EA=8, ft=[128] * 8, gated=False, topk=2),
       dict(E=8, EA=8, ft=[], gated=False, topk=2),
       dict(E=16, EA=17, ft=[128, 128, 96], gated=True, topk=2)]


class Count:

    def __init__(self, sem, n=0):
        self.sem, self.n, self.it, self.per, self.first = sem, n, None, 0, 0

    def loop(self, it, first, per):
        self.it, self.first, self.per, self.start = it, first, per, self.n

    def end(self, trips):
        assert self.n - self.start == self.per, (self.sem, self.n - self.start, self.per)
        self.n, self.it = self.start + trips * self.per, None

    def step(self, more=1):
        self.n += more

    def at(self, back=0):
        v = self.n - back
        assert v > 0, self.sem
        return v if self.it is None or self.per == 0 else (self.it - self.first) * self.per + v


def chunk_of(n, parts):
    return [n * i // parts for i in range(parts + 1)]


def side_schedule(g, hpg, first, last):
    units = hpg * TPQ
    nxt1 = not (last and g == NG - 1)
    nxt2 = not (last and g >= NG - 2)
    half = units * 3 // 8
    late = [("max", (g + 1) % NG, u, c) for u in range(half, units) for c in range(4)] if nxt1 else []
    early = [("max", (g + 2) % NG, u, c) for u in range(half) for c in range(4)] if nxt2 else []
    jobs = late + early[:6] + ([("turn", (g + 1) % NG)] if nxt1 else []) + early[6:]
    spread = NK if nxt2 else NK - 3
    cut = chunk_of(len(jobs), spread) + [len(jobs)] * (NK - spread)
    slots = [jobs[cut[k]:cut[k + 1]] for k in range(NK)]
    if not (first and g == 0):
        slots[2].append(("den", (g - 1) % NG))
        slots[5].append(("spread", (g - 1) % NG))
        if g == 0:
            for i in range(TPQ):
                slots[6 + i].append(("out", i))
    return slots


def max_jobs(g, hpg, lo, hi):
    return [("max", g, u, c) for u in range(lo, hi) for c in range(4)]


def side_prologue(hpg):
    units = hpg * TPQ
    return max_jobs(0, hpg, 0, units) + [("turn", 0)] + max_jobs(1, hpg, 0, units * 3 // 8)


def build(nc, A, out):
    f32, bf16, u8 = mybir.dt.float32, mybir.dt.bfloat16, mybir.dt.uint8
    u32, i32 = mybir.dt.uint32, mybir.dt.int32
    ALU, ACT, AX = mybir.AluOpType, mybir.ActivationFunctionType, mybir.AxisListType

    q_parts = nc.dram_tensor("q_parts", [3, D, T], bf16, kind="Internal").ap()
    k_parts = nc.dram_tensor("k_parts", [3, D, S], bf16, kind="Internal").ap()
    x_place = nc.dram_tensor("x_place", [PLACES, D], f32, kind="Internal").ap()
    y_place = nc.dram_tensor("y_place", [PLACES, D], f32, kind="Internal").ap()
    m_parts = nc.dram_tensor("m_parts", [4, NG * TPQ * P], bf16, kind="Internal").ap()

    ctx = ExitStack()
    with ctx:
        def sb(name, shape, dt=f32, stack=ctx):
            return stack.enter_context(nc.sbuf_tensor(name, shape, dt))

        def sem(name):
            return ctx.enter_context(nc.semaphore(name))

        X = sb("x_res", [P, NT, D])
        xnT = sb("xn_t", [P, 2, T])
        C0 = sb("ctx_a", [P, S])
        C1 = sb("ctx_b", [DC - P + 1, S])
        ident = sb("ident", [P, P])
        sel16 = sb("sel16", [P, 4])
        sel32 = sb("sel32", [P, 4])
        mask_u8 = sb("mask_u8", [P, NK], u8)
        mask_row_u8 = sb("mask_row_u8", [1, S], u8)
        mask_col = sb("mask_col", [P, NK])
        mask_row = sb("mask_row", [1, S], bf16)
        zero_col = sb("zero_col", [P, 1])
        zero_row = sb("zero_row", [1, S], bf16)
        warm = sb("warm", [P, 1])
        ones_row = sb("ones_row", [1, 4, Q], bf16)
        stat = sb("stat", [P, NT, 6])
        mv = sb("mv", [P, NT, 2])
        rstd = sb("rstd", [P, NT])
        WQ = sb("wq", [P, 2, D])
        BQ = sb("bq", [P, 2])
        BQS = sb("bq_scaled", [P, 2])
        WK0 = sb("wk0", [P, D])
        WK1 = sb("wk1", [DC - P + 1, D])
        WV0 = sb("wv0", [P, D])
        WV1 = sb("wv1", [DC - P + 1, D])
        WO = sb("wo", [P, NG, D])

        att = ExitStack()
        with att:
            KS = sb("k_stack", [100, 16, S], bf16, att)
            V = sb("v", [P, NK, 512], f32, att)
            PR = [sb(f"probs{i}", [P, 2, Q], f32, att) for i in range(4)]
            QS = [sb(f"q_stack{i}", [100, 4, Q], bf16, att) for i in range(4)]
            OS = [sb(f"o_sum{i}", [P, Q], f32, att) for i in range(2)]
            RD = sb("recip", [P, 16], f32, att)
            RDX = sb("recip_wide", [P, Q], f32, att)
            OT = sb("o_t", [P, NG, Q], f32, att)
            MX4 = [sb(f"mx4_{i}", [P, 16, 4], f32, att) for i in range(2)]
            MX = [sb(f"mx{i}", [P, 16], f32, att) for i in range(2)]
            MN = sb("m_neg", [16, P], f32, att)
            MR = sb("m_rest", [16, P], f32, att)
            MP = sb("m_part", [16, 4, P], bf16, att)
        prj = ExitStack()
        with prj:
            sb("skip", [100, 16, S], bf16, prj)
            sb("skip_v", [P, NK, 512], f32, prj)
            QK = [sb(f"qk{i}", [P, Q], f32, prj) for i in range(2)]
            QR = [sb(f"qk_rest{i}", [P, Q], f32, prj) for i in range(2)]
            QP = [sb(f"qk_part{i}", [P, 3, Q], bf16, prj) for i in range(4)]
        tab, dense, routing, all_l1 = ExitStack(), ExitStack(), ExitStack(), ExitStack()
        with tab:
            comb = sb("comb", [P, NT, 20], f32, tab)
            first_place = sb("first_place", [P, 16], f32, tab)
            WR = [sb(f"weight_rank{r}", [P, NT], f32, tab) for r in range(2)]
            IP = [sb(f"place_rank{r}", [P, NT], f32, tab) for r in range(2)]
            IS = [sb(f"scatter_rank{r}", [P, NT], u32, tab) for r in range(2)]
            IG = [sb(f"gather_rank{r}", [P, NT], u32, tab) for r in range(2)]
            zeros = sb("zeros", [P, D], f32, tab)
            B2 = sb("b2", [8, D], f32, tab)
            count_up = sb("count_up", [P, TILES], f32, tab)
            NE = sb("expert_tiles", [P, 8], f32, tab)
            EB = sb("expert_begin", [P, 8], f32, tab)
            EE = sb("expert_end", [P, 8], f32, tab)
            TF = sb("tile_expert", [P, TILES], f32, tab)
            TE = sb("tile_expert_i", [P, TILES], i32, tab)
            TM = sb("tile_match", [P, TILES], f32, tab)
            TB = sb("tile_match_bias", [P, TILES, 8], f32, tab)
            BT = sb("tile_bias", [P, TILES, 8], f32, tab)
            B1 = sb("b1", [P, 8, 8], f32, tab)
            with dense:
                WU = [sb(f"w_up{i}", [P, 2 * 2 * 352], f32, dense) for i in range(2)]
                WD = [sb(f"w_down{i}", [P, 3, D], f32, dense) for i in range(2)]
                HT = [sb(f"h_t{i}", [P, 3, Q], f32, dense) for i in range(2)]
                SG = [sb(f"silu_gate{i}", [P, Q], f32, dense) for i in range(2)]
                XE = [sb(f"x_expert{i}", [P, CT, D], f32, dense) for i in range(2)]
                XT = [sb(f"x_expert_t{i}", [P, 2, CAP], f32, dense) for i in range(2)]
                YE = [sb(f"y_expert{i}", [P, CT, D], f32, dense) for i in range(2)]
                YG = [sb(f"y_token{i}", [P, D], f32, dense) for i in range(4)]
            with routing:
                sb("skip_early", [P, EARLY, 4 * NF], f32, routing)
                GW = sb("gate_w", [P, 2, 16], f32, routing)
                GB = sb("gate_b", [P, 16], f32, routing)
                combT = sb("comb_t", [8, T], f32, routing)
                LG = sb("logits", [P, NT, 16], f32, routing)
                PB = sb("prob", [P, NT, 16], f32, routing)
                SL = sb("sel", [P, NT, 16], f32, routing)
                MK = sb("masked", [P, NT, 16], f32, routing)
                RK = sb("rank", [P, NT, 16], f32, routing)
                T4 = [sb(f"t4_{i}", [P, NT, 4], f32, routing) for i in range(6)]
                R1 = sb("r1", [P, NT], f32, routing)
                BIG = [sb(f"big{i}", [P, 16, 16], f32, routing) for i in range(2)]
                less = sb("less", [P, 16, 16], f32, routing)
                tri = sb("tri", [P, P], f32, routing)
                ones = sb("ones", [P, P], f32, routing)
                TOT = sb("totals", [P, NT + 1, 16], f32, routing)
                POS = sb("place", [P, NT, 16], f32, routing)
                WI = sb("within", [P, NT, 16], f32, routing)
                XN = sb("xn", [P, NT, D], f32, routing)
            with all_l1:
                WA = sb("w_all", [P, 8, 2 * NF + NF // P * D], f32, all_l1)

        HA = xnT[:, 0, 0:NF]
        HB = xnT[:, 0, NF:2 * NF]
        XE1 = [xnT[:, 1, i * D:(i + 1) * D] for i in range(2)]
        XT1 = [xnT[:, 1, (2 + i) * D:(3 + i) * D] for i in range(2)]
        YE1 = [xnT[:, 1, (4 + i) * D:(5 + i) * D] for i in range(2)]
        YG1 = [xnT[:, 0, i * D:(i + 1) * D] for i in range(4)]

        PS = ctx.enter_context(nc.psum_tensor("ps", [P, 8, 512], f32))

        s_fence = sem("s_fence")
        s_in = sem("s_in")
        s_const = sem("s_const")
        s_wpad = sem("s_wpad")
        s_wa = sem("s_wa")
        s_stat = sem("s_stat")
        s_std = sem("s_std")
        s_xn = sem("s_xn")
        s_xt = sem("s_xt")
        s_xtc = sem("s_xtc")
        s_v = sem("s_v")
        s_pj = sem("s_pj")
        s_pc = sem("s_pc")
        s_p1 = sem("s_p1")
        s_pp = sem("s_pp")
        s_pd = [sem(f"s_pd{i}") for i in range(4)]
        s_bq = sem("s_bq")
        s_vj = sem("s_vj")
        s_vc = sem("s_vc")
        s_ks = sem("s_ks")
        s_ql = [sem(f"s_ql{i}") for i in range(4)]
        s_md = sem("s_md")
        s_mr = sem("s_mr")
        s_sc = sem("s_sc")
        s_pr = sem("s_pr")
        s_pv = sem("s_pv")
        s_os = sem("s_os")
        s_ot = sem("s_ot")
        s_rd = sem("s_rd")
        s_rx = sem("s_rx")
        s_sj = sem("s_sj")
        s_sf = sem("s_sf")
        s_mx = sem("s_mx")
        s_mp = sem("s_mp")
        s_gl = sem("s_gl")
        s_lg = sem("s_lg")
        s_lc = sem("s_lc")
        s_ex = sem("s_ex")
        s_cb = sem("s_cb")
        s_ct = sem("s_ct")
        s_ctc = sem("s_ctc")
        s_by = sem("s_by")
        s_w = [sem(f"s_w{i}") for i in range(2)]
        s_h = sem("s_h")
        s_sg = sem("s_sg")
        s_hr = sem("s_hr")
        s_y = sem("s_y")
        s_yf = sem("s_yf")
        s_z = sem("s_z")
        s_ix = sem("s_ix")
        s_px = sem("s_px")
        s_xe = [sem(f"s_xe{i}") for i in range(2)]
        s_tr = sem("s_tr")
        s_te = sem("s_te")
        s_yc = sem("s_yc")
        s_yd = [sem(f"s_yd{i}") for i in range(2)]
        s_yg = [sem(f"s_yg{i}") for i in range(4)]
        s_we = [sem(f"s_we{e}") for e in range(8)]
        s_wr = sem("s_wr")
        s_ti = sem("s_ti")
        s_up = sem("s_up")
        s_uc = sem("s_uc")
        s_ut = sem("s_ut")
        s_ge = sem("s_ge")
        s_out = sem("s_out")

        HR_FREE, YF_FREE, Y_FREE = 4, 4, 2 * TPQ

        block = ctx.enter_context(nc.Block())

        def fence(eng, n):
            n[0] += 1
            eng.drain().then_inc(s_fence, 1)
            eng.wait_ge(s_fence, 5 * n[0])

        def key_rows(k):
            return P if k < NK - 1 else KREM

        @block.sync
        def _(sp):
            fences = [0]
            wpad, pp = Count(s_wpad), Count(s_pp)
            pd = [Count(s) for s in s_pd]
            mp, md, pv = Count(s_mp), Count(s_md), Count(s_pv)
            wf = Count(s_y, Y_FREE)
            px, yc, tr = Count(s_px), Count(s_yc), Count(s_tr)

            def load_attention_weights(L):
                a = ATT[L]
                dh, pw, hpg = a["dh"], a["pw"], a["hpg"]
                H = D // dh
                n = 0
                wpad.step()
                sp.wait_ge(s_wpad, wpad.at())
                loads = [(WQ[:], A[f"wq{L}"].rearrange("(k p) n -> p k n", p=P)),
                         (WK0[:], A[f"wk{L}"][0:P, :]), (WK1[0:DC - P, :], A[f"wk{L}"][P:DC, :]),
                         (WV0[:], A[f"wv{L}"][0:P, :]), (WV1[0:DC - P, :], A[f"wv{L}"][P:DC, :])]
                for j in range(hpg):
                    loads.append((WO[pw * j:pw * j + dh, :, :],
                                  A[f"wo{L}"].rearrange("(g j d) n -> j d g n", g=NG, j=hpg)[j]))
                if L < 3:
                    loads += [(BQ[:], A[f"bq{L}"].rearrange("(m p) -> p m", p=P)),
                              (WK1[DC - P:DC - P + 1, :], A[f"bk{L}"].rearrange("(a n) -> a n", a=1)),
                              (WV1[DC - P:DC - P + 1, :], A[f"bv{L}"].rearrange("(a n) -> a n", a=1)),
                              (WO[dh:dh + 1, 0, :], A[f"bo{L}"].rearrange("(a n) -> a n", a=1))]
                for dst, src in loads:
                    sp.dma_start(dst, src, allow_slow_non_contiguous=True).then_inc(s_wa, 16)

            def load_constant_rows(L):
                ones_flat = ones_row[:].rearrange("p a b -> p (a b)")[:, 0:S]
                for row, src in ((96, mask_row[:] if L == 3 else zero_row[:]), (97, ones_flat), (98, ones_flat),
                                 (99, ones_flat)):
                    sp.dma_start(KS[row:row + 1, :, :], src.unsqueeze(1).to_broadcast([1, 16, S]))\
                      .then_inc(s_ks, 16)

            def load_keys(L, half, third):
                dh, nsub = ATT[L]["dh"], ATT[L]["nsub"]
                nh = D // dh // 2
                for row in (2 * third, 2 * third + 1):
                    part = [0, 1, 2, 0, 1, 0][row]
                    src = k_parts[part].rearrange("(h d) s -> d h s", d=dh)[:, half * nh:(half + 1) * nh, :]
                    r, sub = (row, 0) if nsub == 1 else (row % 3, row // 3)
                    sp.dma_start(KS[r * dh:(r + 1) * dh, half * 8 + sub:half * 8 + 8:nsub, :], src)\
                      .then_inc(s_ks, 16)

            def load_queries(L, t, buf):
                a = ATT[L]
                dh, hpg = a["dh"], a["hpg"]
                c, g = (t, 0) if isinstance(t, int) else t
                cols = bass.ts(c, Q)
                dst = QS[buf]
                if a["nsub"] == 1:
                    for row, part in enumerate([0, 0, 0, 1, 1, 2]):
                        src = q_parts[part].rearrange("(h d) t -> d h t", d=dh)[:, g * hpg:(g + 1) * hpg, cols]
                        sp.dma_start(dst[row * dh:(row + 1) * dh, :, :], src).then_inc(s_ql[buf], 16)
                else:
                    for row, part in enumerate([0, 0, 0, 1, 1, 2]):
                        src = q_parts[part].rearrange("(h d) t -> d h t", d=dh)[:, g * hpg:(g + 1) * hpg, cols]
                        r = row % 3
                        sp.dma_start(dst[r * dh:(r + 1) * dh, row // 3::2, :], src).then_inc(s_ql[buf], 16)
                sp.dma_start(dst[96:97, :, :], ones_row[:]).then_inc(s_ql[buf], 16)

            def store_max_rows(L, g):
                a = ATT[L]
                units = a["hpg"] * TPQ
                mp.step()
                sp.wait_ge(s_mp, mp.at())
                m_dst = m_parts[:, 0:units * P].rearrange("r (u x) -> u r x", u=units)
                sp.dma_start(m_dst, MP[0:units, :, :]).then_inc(s_md, 16)
                md.step(16)
                if md.n > 0:
                    sp.wait_ge(s_md, md.at())
                src = m_parts[:, 0:units * P].rearrange("r (j x) -> r j x", x=Q)
                sp.dma_start(QS[g][96:100, 0:4:a["nsub"], :], src).then_inc(s_mr, 16)

            sp.dma_start(X[:], A["x"].rearrange("(t p) d -> p t d", p=P)).then_inc(s_in, 16)
            sp.dma_start(C0[:], A["ctx_t"][0:P, :]).then_inc(s_in, 16)
            sp.dma_start(C1[0:DC - P, :], A["ctx_t"][P:DC, :]).then_inc(s_in, 16)
            sp.dma_start(mask_u8[:, 0:NK - 1], A["mask"][:, 0:P * (NK - 1)].rearrange("a (k p) -> p (a k)", p=P),
                         allow_slow_non_contiguous=True).then_inc(s_in, 16)
            sp.dma_start(mask_u8[0:KREM, NK - 1:NK], A["mask"][:, P * (NK - 1):S].rearrange("a p -> p a"),
                         allow_slow_non_contiguous=True).then_inc(s_in, 16)
            sp.dma_start(mask_row_u8[:], A["mask"]).then_inc(s_in, 16)
            load_attention_weights(0)
            fence(sp, fences)

            for L in range(4):
                a = ATT[L]
                fence(sp, fences)
                load_constant_rows(L)
                for u in range(16):
                    kind, m, c = 1 - u // 8, (u // 4) % 2, u % 4
                    pp.step()
                    sp.wait_ge(s_pp, pp.at())
                    if u in (4, 8):
                        for i in range(4):
                            sp.wait_ge(s_pd[i], pd[i].at())
                    n = Q if kind == 0 else min(Q, S - c * Q)
                    where = q_parts if kind == 0 else k_parts
                    dst = where[:, m * P:(m + 1) * P, c * Q:c * Q + n].rearrange("r p t -> p r t")
                    sp.dma_start(dst, QP[u % 4][:, :, 0:n]).then_inc(s_pd[u % 4], 16)
                    pd[u % 4].step(16)
                    if u in (4, 5, 6, 8, 9, 10):
                        load_keys(L, u // 8, u % 4)
                for i in range(4):
                    sp.wait_ge(s_pd[i], pd[i].at())
                fence(sp, fences)

                for g in range(3):
                    load_queries(L, (0, g), g)
                store_max_rows(L, 0)

                pairs = NK * a["hpg"] // 2

                def iteration(it, first, last):
                    for g in range(NG):
                        if not (first and g == 0):
                            pv.step(pairs)
                        if not (last and g > 0):
                            if not (first and g == 0):
                                sp.wait_ge(s_pv, pv.at())
                            load_queries(L, (it, 3) if g == 0 else (it + 1, g - 1), (g + 3) % 4)
                        if not (last and g == NG - 1):
                            store_max_rows(L, (g + 1) % NG)

                iteration(0, True, False)
                with sp.Fori(1, NQ - 1) as it:
                    for c, per in ((mp, 4), (md, 64), (pv, NG * pairs)):
                        c.loop(it, 1, per)
                    iteration(it, False, False)
                    for c in (mp, md, pv):
                        c.end(NQ - 2)
                iteration(NQ - 1, False, True)
                pv.step(pairs)
                fence(sp, fences)

                f = FFN[L]
                E = f["E"]
                if L < 3:
                    load_attention_weights(L + 1)
                sp.dma_start(GW[:, :, 0:E], A[f"gw{L}"].rearrange("(k p) e -> p k e", p=P),
                             allow_slow_non_contiguous=True).then_inc(s_gl, 16)
                if L >= 2:
                    sp.dma_start(GB[:, 0:E], A[f"gb{L}"].partition_broadcast(P)).then_inc(s_gl, 16)
                if L in (1, 2):
                    sp.dma_start(B2[:], A[f"b2_{L}"]).then_inc(s_gl, 16)
                if L == 1:
                    sp.dma_start(B1[:], A["b1"].rearrange("e p f -> p e f"),
                                 allow_slow_non_contiguous=True).then_inc(s_gl, 16)
                    for e in range(EARLY):
                        sp.dma_start(WA[:, e, 0:2 * NF], A["up1"][e]).then_inc(s_we[e], 16)
                        sp.dma_start(WA[:, e, 2 * NF:], A["down1"][e]).then_inc(s_we[e], 16)

                def load_expert(e, par):
                    def at(name):
                        return A[name][bass.ds(e, 1)].rearrange("a p x -> (a p) x")
                    if L == 2:
                        sp.dma_start(WU[par][:, 0:1024], at("we2")).then_inc(s_w[par], 16)
                        return
                    F = sum(f["ft"]) * (2 if f["gated"] else 1)
                    sp.dma_start(WU[par][:, 0:2 * F], at(f"up{L}")).then_inc(s_w[par], 16)
                    full = sum(1 for r in f["ft"] if r == P)
                    sp.dma_start(WD[par][:, 0:full, :].rearrange("p f n -> p (f n)"), at(f"down{L}")).then_inc(s_w[par], 16)
                    if f["gated"]:
                        sp.dma_start(WD[par][0:96, 2, :], at("down3b")).then_inc(s_w[par], 16)

                items = f["EA"] if L != 2 else 4
                fence(sp, fences)
                if L in (0, 2):
                    for par in range(2):
                        load_expert(par, par)
                    with sp.Fori(1, items // 2) as i:
                        wf.loop(i, 1, 2 * NT)
                        for par in range(2):
                            wf.step(NT)
                            sp.wait_ge(s_y, wf.at())
                            load_expert(i * 2 + par, par)
                        wf.end(items // 2 - 1)
                    wf.step(2 * NT)
                elif L == 1:
                    x_tile = x_place.rearrange("(i p) d -> i p d", p=P)
                    y_tile = y_place.rearrange("(i p) d -> i p d", p=P)

                    def load_tile(i, par):
                        sp.dma_start(XE1[par], x_tile[bass.ds(i, 1)].rearrange("a p d -> (a p) d"))\
                          .then_inc(s_xe[par], 16)

                    def store_tile(i, par):
                        yc.step()
                        sp.wait_ge(s_yc, yc.at())
                        sp.dma_start(y_tile[bass.ds(i, 1)].rearrange("a p d -> (a p) d"), YE1[par])\
                          .then_inc(s_yd[par], 16)

                    px.step(2 * NT * 16)
                    sp.wait_ge(s_px, px.at())
                    def next_tile(i, par):
                        tr.step()
                        sp.wait_ge(s_tr, tr.at())
                        load_tile(i, par)

                    load_tile(0, 0)
                    load_tile(1, 1)
                    next_tile(2, 0)
                    with sp.Fori(0, TILES // 2 - 1) as i:
                        loops = ((yc, 2), (tr, 2))
                        for c, per in loops:
                            c.loop(i, 0, per)
                        for par in range(2):
                            next_tile(i * 2 + (3 + par), 1 - par)
                            store_tile(i * 2 + par, par)
                        for c, per in loops:
                            c.end(TILES // 2 - 1)
                    for j in range(TILES - 3, TILES):
                        store_tile(j, j % 2)
                    tr.step(2)
                    wf.step(TILES)
                else:
                    load_expert(16, 0)
                    load_expert(0, 1)
                    px.step(2 * NT * 16)
                    sp.wait_ge(s_px, px.at())

                    def load_rows(e, par):
                        rows = x_place.rearrange("(e r) d -> e r d", r=CAP)[bass.ds(e, 1)].rearrange("a r d -> (a r) d")
                        full = (CT - 1) * P
                        sp.dma_start(XE[par][:, 0:CT - 1, :], rows[0:full, :].rearrange("(t p) d -> p t d", p=P))\
                          .then_inc(s_xe[par], 16)
                        sp.dma_start(XE[par][0:CLAST, CT - 1, :], rows[full:CAP, :]).then_inc(s_xe[par], 16)

                    def store_answers(e, par):
                        rows = y_place.rearrange("(e r) d -> e r d", r=CAP)[bass.ds(e, 1)].rearrange("a r d -> (a r) d")
                        full = (CT - 1) * P
                        sp.dma_start(rows[0:full, :].rearrange("(t p) d -> p t d", p=P), YE[par][:, 0:CT - 1, :])\
                          .then_inc(s_yd[par], 16)
                        sp.dma_start(rows[full:CAP, :], YE[par][0:CLAST, CT - 1, :]).then_inc(s_yd[par], 16)

                    load_rows(0, 0)
                    load_rows(1, 1)
                    wf.step(NT)
                    sp.wait_ge(s_y, wf.at())
                    load_expert(1, 0)

                    def turn(e, par):
                        yc.step(CT)
                        sp.wait_ge(s_yc, yc.at())
                        store_answers(e, par)

                    with sp.Fori(1, 8) as i:
                        loops = ((yc, 2 * CT), (tr, 2))
                        for c, per in loops:
                            c.loop(i, 1, per)
                        for par in range(2):
                            tr.step()
                            sp.wait_ge(s_tr, tr.at())
                            load_rows(i * 2 + par, par)
                            turn(i * 2 - 2 + par, par)
                            load_expert(i * 2 + par, 1 - par)
                        for c, per in loops:
                            c.end(7)
                    for par in range(2):
                        turn(14 + par, par)
                    for c in range(NQ):
                        sp.wait_ge(s_ix, 1 + 2 * NT + 1 + 2 * TPQ * (c + 1))
                        sp.dma_start(out.rearrange("(c t p) d -> c p t d", t=TPQ, p=P)[c],
                                     X[:, c * TPQ:(c + 1) * TPQ, :]).then_inc(s_out, 16)
                fence(sp, fences)
            sp.wait_ge(s_out, 16 * NQ)

        @block.gpsimd
        def _(pool):
            fences = [0]
            n = [0]
            ix, px, z = Count(s_ix), Count(s_px), Count(s_z)
            yd, yf = [Count(q) for q in s_yd], Count(s_yf, YF_FREE)

            def link(ins):
                n[0] += 1
                ins.then_inc(s_const, 1)
                pool.wait_ge(s_const, n[0])

            def clear_attention_weights(L):
                link(pool.memset(WV1[DC - P:DC - P + 1, :], 0.0))
                link(pool.memset(WK1[DC - P:DC - P + 1, :], 0.0))
                link(pool.memset(BQ[:], 0.0))
                pool.memset(WO[:], 0.0).then_inc(s_wpad, 1)

            clear_attention_weights(0)
            link(pool.memset(zero_col[:], 0.0))
            link(pool.memset(zero_row[:], 0.0))
            link(pool.memset(ones_row[:], 1.0))
            link(pool.memset(C1[DC - P:DC - P + 1, :], 1.0))
            link(pool.memset(ident[:], 0.0))
            link(pool.affine_select(out=ident[:], in_=ident[:], compare_op=ALU.not_equal, fill=1.0,
                                    base=0, pattern=[[-1, P]], channel_multiplier=1))
            for m, pw, dh in ((sel16, 32, 16), (sel32, 64, 32)):
                link(pool.memset(m[:], 0.0))
                link(pool.affine_select(out=m[:], in_=m[:], compare_op=ALU.not_equal, fill=1.0, base=-dh,
                                        pattern=[[-pw, 4]], channel_multiplier=1))
            fence(pool, fences)
            for L in range(4):
                dh = ATT[L]["dh"]
                link(pool.memset(V[:], 0.0))
                link(pool.memset(V[:].rearrange("p k (h w) -> p k h w", w=ATT[L]["pw"])[:, :, :, dh:dh + 1], 1.0))
                fence(pool, fences)
                link(pool.memset(MP[:, 0, :], 0.0))
                fence(pool, fences)
                fence(pool, fences)
                if L < 3:
                    clear_attention_weights(L + 1)
                link(pool.memset(less[:], 1.0))
                link(pool.affine_select(out=less[:], in_=less[:], compare_op=ALU.is_gt, fill=0.0,
                                        base=0, pattern=[[1, 16], [-1, 16]], channel_multiplier=0))
                link(pool.memset(ones[:], 1.0))
                link(pool.affine_select(out=tri[:], in_=ones[:], compare_op=ALU.is_gt, fill=0.0,
                                        base=0, pattern=[[1, P]], channel_multiplier=-1))
                link(pool.memset(comb[:], 1.0))
                for e in range(16):
                    link(pool.memset(first_place[:, e:e + 1], float(CAP * e)))
                for i in range(TILES):
                    link(pool.memset(count_up[:, i:i + 1], float(i)))
                if L in (1, 3):
                    link(pool.memset(zeros[:], 0.0))
                    pool.dma_start(x_place.rearrange("(a p) d -> p a d", p=P),
                                   zeros[:].unsqueeze(1).to_broadcast([P, PLACES // P, D])).then_inc(s_z, 16)
                fence(pool, fences)
                if L == 0:
                    yf.step(FFN[0]["EA"] * NT)
                if L in (1, 3):
                    z.step(16)
                    pool.wait_ge(s_z, z.at())
                    ix.step()
                    pool.wait_ge(s_ix, ix.at())
                    for r in range(2):
                        for t in range(NT):
                            pool.indirect_dma_start(x_place, bass.IndirectOffsetOnAxis(ap=IS[r][:, t:t + 1], axis=0),
                                                    XN[:, t, :], None, bounds_check=PLACES - 1,
                                                    oob_is_err=False).then_inc(s_px, 16)
                    px.step(2 * NT * 16)
                    if L == 1:
                        for e in range(EARLY):
                            pool.wait_ge(s_we[e], 32)
                            pool.sem_inc(s_wr, 1)
                        pool.wait_ge(s_px, px.at())
                        yf.step(NT)
                        pool.wait_ge(s_yf, yf.at())
                        for e in range(EARLY, 8):
                            pool.dma_start(WA[:, e, 0:2 * NF], A["up1"][e]).then_inc(s_we[e], 16)
                            pool.dma_start(WA[:, e, 2 * NF:], A["down1"][e]).then_inc(s_we[e], 16)
                        for e in range(EARLY, 8):
                            pool.wait_ge(s_we[e], 32)
                            pool.sem_inc(s_wr, 1)
                        for par in range(2):
                            yd[par].step(16 * (TILES - TILES // 2 if par == 0 else TILES // 2))
                    else:
                        for par in range(2):
                            yd[par].step(8 * 32)
                    for par in range(2):
                        pool.wait_ge(s_yd[par], yd[par].at())
                    yg = YG1 if L == 1 else [q[:] for q in YG]
                    used = TILES * P if L == 1 else PLACES
                    for t in range(NT):
                        for r in range(2):
                            k = 2 * t + r
                            if k >= 4:
                                pool.wait_ge(s_ix, ix.at() + k - 3)
                            pool.indirect_dma_start(yg[k % 4], None, y_place[0:used, :],
                                                    bass.IndirectOffsetOnAxis(ap=IG[r][:, t:t + 1], axis=0))\
                                .then_inc(s_yg[k % 4], 16)
                    ix.step(2 * NT)
                fence(pool, fences)

        @block.scalar
        def _(act):
            act.sem_inc(s_hr, HR_FREE)
            act.sem_inc(s_yf, YF_FREE)
            act.sem_inc(s_y, Y_FREE)
            fences = [0]
            stat_c, xt, xtc = Count(s_stat), Count(s_xt), Count(s_xtc)
            pj, pp, pd, bq = Count(s_pj), Count(s_pp), [Count(q) for q in s_pd], Count(s_bq)
            vj = Count(s_vj)
            sc, pv, o, ot, rd, dv = Count(s_sc), Count(s_pv), Count(s_pv), Count(s_ot), Count(s_rd), Count(s_ot)
            lc, ctc = Count(s_lc), Count(s_ct)
            h, dn, hr = Count(s_h), Count(s_y, Y_FREE), Count(s_hr, HR_FREE)
            tr, ut = Count(s_tr), Count(s_ut)
            fence(act, fences)

            def normalize():
                act.activation(warm[:], zero_col[:], ACT.Sqrt)
                stat_c.step()
                act.wait_ge(s_stat, stat_c.at())
                act.activation(rstd[:], mv[:, :, 1], ACT.Sqrt).then_inc(s_std, 1)
                for c in range(NQ):
                    xt.step()
                    act.wait_ge(s_xt, xt.at())
                    for half in range(2):
                        act.activation(xnT[:, half, c * Q:(c + 1) * Q], PS[:, 2 * (c % 2) + half, :],
                                       ACT.Copy).then_inc(s_xtc, 1)
                fence(act, fences)

            for L in range(4):
                a = ATT[L]
                dh, pw, hpg, nsub = a["dh"], a["pw"], a["hpg"], a["nsub"]
                npair = hpg // 2
                normalize()

                scale = 0.25 if dh == 16 else 32.0 ** -0.5
                for u in range(16):
                    kind, m, c = 1 - u // 8, (u // 4) % 2, u % 4
                    n = Q if kind == 0 else min(Q, S - c * Q)
                    pj.step()
                    act.wait_ge(s_pj, pj.at())
                    if pp.n > 1:
                        act.wait_ge(s_pp, pp.at(1))
                    pp.step()
                    if pd[u % 4].n > 0:
                        act.wait_ge(s_pd[u % 4], pd[u % 4].at())
                    pd[u % 4].step(16)
                    if u == 8:
                        act.activation(BQS[:], BQ[:], ACT.Copy, scale=scale).then_inc(s_bq, 1)
                        bq.step()
                        act.wait_ge(s_bq, bq.at())
                    for dst in (QK[u % 2][:, 0:n], QP[u % 4][:, 0, 0:n]):
                        if kind == 0:
                            last = act.activation(dst, PS[:, u % 4, 0:n], ACT.Identity, bias=BQS[:, m:m + 1], scale=scale)
                        else:
                            last = act.activation(dst, PS[:, u % 4, 0:n], ACT.Copy)
                    last.then_inc(s_pc, 1)
                    if u < NK:
                        vj.step()
                        act.wait_ge(s_vj, vj.at())
                        r = key_rows(u)
                        act.activation(V[0:r, u, :].rearrange("p (h w) -> p h w", w=pw)[:, :, 0:dh],
                                       PS[0:r, 4 + u % 4, 0:D].rearrange("p (h w) -> p h w", w=dh),
                                       ACT.Copy).then_inc(s_vc, 1)
                fence(act, fences)

                pair = [0]

                def exps(k):
                    r = key_rows(k)
                    bias = mask_col if L == 3 else None
                    for j in range(npair):
                        b = pair[0] % 2
                        sc.step()
                        act.wait_ge(s_sc, sc.at())
                        if pv.n > 3:
                            act.wait_ge(s_pv, pv.at(3))
                        pv.step()
                        act.activation(PR[pair[0] % 4][0:r, :, :], PS[0:r, 2 * b:2 * b + 2, :], ACT.Exp,
                                       bias=mask_col[0:r, k:k + 1] if L == 3 else zero_col[0:r, :],
                                       scale=1.0).then_inc(s_pr, 1)
                        pair[0] += 1

                def copy_sums(g):
                    o.step(NK * npair)
                    act.wait_ge(s_pv, o.at())
                    if ot.n > 1:
                        act.wait_ge(s_ot, ot.at(1))
                    ot.step()
                    act.activation(OS[g % 2][:], PS[:, 4, :], ACT.Copy).then_inc(s_os, 1)

                def widen_reciprocals():
                    rd.step()
                    act.wait_ge(s_rd, rd.at())
                    if dv.n > 0:
                        act.wait_ge(s_ot, dv.at(0))
                    dv.step()
                    act.activation(RDX[:, 0:TPQ * P].rearrange("p (a w) -> p a w", w=pw),
                                   RD[:, 0:TPQ * hpg].unsqueeze(2).to_broadcast([P, TPQ * hpg, pw]),
                                   ACT.Copy).then_inc(s_rx, 1)

                def iteration(first):
                    for g in range(NG):
                        for k in range(NK):
                            exps(k)
                            if k == 0 and not (first and g == 0):
                                copy_sums((g - 1) % NG)
                            if k == 3 and not (first and g == 0):
                                widen_reciprocals()

                iteration(True)
                with act.Fori(1, NQ - 1) as it:
                    n = NG * NK * npair
                    for c, per in ((sc, n), (pv, n), (o, n), (ot, NG), (rd, NG), (dv, NG)):
                        c.loop(it, 1, per)
                    iteration(False)
                    for c in (sc, pv, o, ot, rd, dv):
                        c.end(NQ - 2)
                iteration(False)
                copy_sums(NG - 1)
                widen_reciprocals()
                fence(act, fences)

                f = FFN[L]
                E, ft = f["E"], f["ft"]
                normalize()
                lc.step()
                act.wait_ge(s_lc, lc.at())
                act.activation(PB[:, :, 0:E], LG[:, :, 0:E], ACT.Sigmoid if L == 0 else ACT.Exp).then_inc(s_ex, 1)
                if L in (1, 2):
                    for c in range(NQ):
                        ctc.step()
                        act.wait_ge(s_ct, ctc.at())
                        act.activation(combT[:, c * Q:(c + 1) * Q], PS[0:8, c % 2, :], ACT.Copy).then_inc(s_ctc, 1)
                if L == 2:
                    dn.step(4 * NT)
                elif L == 1:
                    def gelu_tile(i, par):
                        ut.step()
                        act.wait_ge(s_ut, ut.at())
                        for q in range(NF // P):
                            last = act.activation(HB[:, q * P:(q + 1) * P], PS[:, 2 + q // 4, q % 4 * P:(q % 4 + 1) * P],
                                                  ACT.Gelu, bias=BT[:, bass.ds(i, 1), q], scale=1.0)
                        last.then_inc(s_ge, 1)

                    with act.Fori(0, TILES // 2) as i:
                        ut.loop(i, 0, 2)
                        for par in range(2):
                            gelu_tile(i * 2 + par, par)
                        ut.end(TILES // 2)
                    gelu_tile(TILES - 1, 0)
                    tr.step(TILES)
                    dn.step(TILES)
                else:
                    job = [0]

                    def expert(par):
                        for c in range(NQ):
                            for t, rows in enumerate(ft):
                                h.step()
                                act.wait_ge(s_h, h.at())
                                if f["gated"]:
                                    if hr.n > 1:
                                        act.wait_ge(s_hr, hr.at(1))
                                    hr.step()
                                    act.activation(SG[job[0] % 2][0:rows, :], PS[0:rows, 2 * (job[0] % 2), :],
                                                   ACT.Silu).then_inc(s_sg, 1)
                                else:
                                    if t == 0:
                                        if dn.n > TPQ:
                                            act.wait_ge(s_y, dn.at(TPQ))
                                        dn.step(TPQ)
                                    act.activation(HT[c % 2][:, t, :], PS[:, job[0] % 4, :],
                                                   ACT.Silu).then_inc(s_hr, 1)
                                job[0] += 1

                    if L == 3:
                        expert(0)
                        dn.step(NT)
                    EA = f["EA"]
                    if L < 3:
                        loops = ((h, 2 * NQ * len(ft)), (dn, 2 * NT))
                        with act.Fori(0, EA // 2) as i:
                            for c, per in loops:
                                c.loop(i, 0, per)
                            expert(0)
                            expert(1)
                            for c, per in loops:
                                c.end(EA // 2)
                        hr.step(EA * NQ * len(ft))
                    else:
                        def routed(par):
                            tr.step()
                            act.wait_ge(s_tr, tr.at())
                            act.activation(XT[par][:], PS[:, 6:8, 0:CAP], ACT.Copy).then_inc(s_te, 1)
                            for t, rows in enumerate(ft):
                                h.step()
                                act.wait_ge(s_h, h.at())
                                act.wait_ge(s_hr, hr.at(1))
                                hr.step()
                                act.activation(SG[job[0] % 2][0:rows, 0:CAP],
                                               PS[0:rows, 2 * (job[0] % 2), 0:CAP], ACT.Silu).then_inc(s_sg, 1)
                                job[0] += 1

                        loops = ((h, 2 * len(ft)), (hr, 2 * len(ft)), (tr, 2))
                        with act.Fori(0, 8) as i:
                            for c, per in loops:
                                c.loop(i, 0, per)
                            routed(0)
                            routed(1)
                            for c, per in loops:
                                c.end(8)
                fence(act, fences)

        @block.vector
        def _(dve):
            fences = [0]
            v = Count(s_v)
            std, xn = Count(s_std), Count(s_xn)
            pc = Count(s_pc)
            sj, md = Count(s_sj), Count(s_md)
            os_ = Count(s_os)
            lg, ex = Count(s_lg), Count(s_ex)
            gl = Count(s_gl)
            by = Count(s_by)
            h, sg, dn, y, yf = Count(s_h), Count(s_sg), Count(s_y, Y_FREE), Count(s_y, Y_FREE), Count(s_yf, YF_FREE)
            sf, rx = Count(s_sf), Count(s_rx)
            yd = [Count(q) for q in s_yd]
            ix, yg = Count(s_ix), [Count(q) for q in s_yg]
            up, tr = Count(s_up), Count(s_tr)

            def link(ins):
                ins.then_inc(s_v, 1)
                v.step()
                dve.wait_ge(s_v, v.at())

            dve.wait_ge(s_in, 6 * 16)
            link(dve.memset(mask_col[:], 0.0))
            for r, lo, hi in ((P, 0, NK - 1), (KREM, NK - 1, NK)):
                link(dve.tensor_copy(mask_col[0:r, lo:hi], mask_u8[0:r, lo:hi]))
                link(dve.tensor_scalar(mask_col[0:r, lo:hi], mask_col[0:r, lo:hi], 1.0, -MASKED,
                                       ALU.subtract, ALU.mult))
            link(dve.tensor_scalar(mask_row[:], mask_row_u8[:], 1.0, -MASKED, ALU.subtract, ALU.mult))
            fence(dve, fences)

            def normalize(keep=False, counted=False):
                if not counted:
                    for t in range(NT):
                        last = dve.bn_stats(stat[:, t, :], X[:, t, :])
                    link(last)
                for t in range(NT):
                    last = dve.bn_aggr(mv[:, t, :], stat[:, t, :])
                link(last)
                dve.tensor_scalar(mv[:, :, 1], mv[:, :, 1], EPS, None, ALU.add).then_inc(s_stat, 1)
                std.step()
                dve.wait_ge(s_std, std.at())
                link(dve.reciprocal(rstd[:], rstd[:]))
                for c in range(NQ):
                    for i in range(TPQ):
                        t = c * TPQ + i
                        last = dve.tensor_scalar(XN[:, t, :], X[:, t, :], mv[:, t, 0:1], rstd[:, t:t + 1],
                                                 ALU.subtract, ALU.mult)
                    last.then_inc(s_xn, 1)
                    xn.step()
                    if keep:
                        dve.wait_ge(s_xn, xn.at())
                        tiles = X[:, c * TPQ:(c + 1) * TPQ, :]
                        link(dve.tensor_tensor(tiles, tiles, XN[:, c * TPQ:(c + 1) * TPQ, :], ALU.add))
                fence(dve, fences)

            for L in range(4):
                a = ATT[L]
                dh, pw, hpg, nsub = a["dh"], a["pw"], a["hpg"], a["nsub"]
                units = hpg * TPQ
                normalize(counted=L == 2)

                for u in range(16):
                    kind, c = 1 - u // 8, u % 4
                    n = Q if kind == 0 else min(Q, S - c * Q)
                    x, r, p = QK[u % 2][:, 0:n], QR[u % 2][:, 0:n], QP[u % 4]
                    pc.step()
                    dve.wait_ge(s_pc, pc.at())
                    link(dve.tensor_tensor(r, x, p[:, 0, 0:n], ALU.subtract))
                    link(dve.tensor_copy(p[:, 1, 0:n], r))
                    dve.tensor_tensor(p[:, 2, 0:n], r, p[:, 1, 0:n], ALU.subtract).then_inc(s_pp, 1)
                fence(dve, fences)

                njob = [0]

                nd = TPQ * hpg

                def side(job, it):
                    bank = 5 + njob[0] % 3
                    njob[0] += 1
                    sj.step()
                    if job[0] == "turn":
                        if md.n > 0:
                            dve.wait_ge(s_md, md.at())
                        md.step(16)
                    dve.wait_ge(s_sj, sj.at())
                    if job[0] == "max":
                        _, g, u, c = job
                        ins = dve.reduce_max(MX4[g % 2][:, u, c:c + 1], PS[:, bank, 0:CK[c]], AX.X)
                        ins.then_inc(s_sf, 1)
                        if u == units - 1 and c == 3:
                            dve.wait_ge(s_sf, sf.at())
                            dve.reduce_max(MX[g % 2][:, 0:units], MX4[g % 2][:, 0:units, :], AX.X).then_inc(s_mx, 1)
                    elif job[0] == "turn":
                        neg, rest = MN[0:units, :], MR[0:units, :]
                        dve.tensor_scalar(neg, PS[0:units, bank, 0:P], -1.0, None, ALU.mult).then_inc(s_sf, 1)
                        dve.wait_ge(s_sf, sf.at())
                        link(dve.tensor_copy(MP[0:units, 1, :], neg))
                        link(dve.tensor_tensor(rest, neg, MP[0:units, 1, :], ALU.subtract))
                        link(dve.tensor_copy(MP[0:units, 2, :], rest))
                        dve.tensor_tensor(MP[0:units, 3, :], rest, MP[0:units, 2, :], ALU.subtract).then_inc(s_mp, 1)
                    elif job[0] == "den":
                        g = job[1]
                        if rx.n > 0:
                            dve.wait_ge(s_rx, rx.at(0))
                        rx.step()
                        dve.reciprocal(RD[:, 0:nd], PS[:, bank, 0:nd]).then_inc(s_sf, 1)
                        dve.wait_ge(s_sf, sf.at())
                        dve.sem_inc(s_rd, 1)
                    elif job[0] == "spread":
                        g = job[1]
                        dve.tensor_tensor(OT[:, g, :], OS[g % 2][:], PS[:, bank, :], ALU.mult).then_inc(s_sf, 1)
                        dve.wait_ge(s_sf, sf.at())
                        dve.sem_inc(s_ot, 1)
                    else:
                        t = (it - 1) * TPQ + job[1]
                        x = X[:, bass.ds(t, 1), :].rearrange("p a d -> p (a d)") if not isinstance(t, int) else X[:, t, :]
                        dve.tensor_tensor(x, x, PS[:, bank, 0:D], ALU.add).then_inc(s_sf, 1)

                def sides(jobs, it):
                    for job in jobs:
                        sf.step()
                        side(job, it)

                sides(side_prologue(hpg), 0)

                def iteration(it, first, last):
                    njob[0] = 0
                    for g in range(NG):
                        for k, slot in enumerate(side_schedule(g, hpg, first, last)):
                            sides(slot, it)
                            if last and g == NG - 1 and k < NT - TPQ:
                                if k == 0:
                                    dve.wait_ge(s_sf, sf.at())
                                dve.bn_stats(stat[:, k, :], X[:, k, :])

                per = sum(len(s) for g in range(NG) for s in side_schedule(g, hpg, False, False))
                iteration(0, True, False)
                with dve.Fori(1, NQ - 1) as it:
                    loops = ((sj, per), (sf, per), (md, 64), (v, 4 * 3), (rx, NG))
                    for c, p in loops:
                        c.loop(it, 1, p)
                    iteration(it, False, False)
                    for c, p in loops:
                        c.end(NQ - 2)
                iteration(NQ - 1, False, True)
                njob[0] = 0
                sides([("den", NG - 1), ("spread", NG - 1)] + [("out", i) for i in range(TPQ)], NQ)
                dve.wait_ge(s_sf, sf.at())
                for t in range(NT - TPQ, NT):
                    dve.bn_stats(stat[:, t, :], X[:, t, :])
                fence(dve, fences)

                f = FFN[L]
                E, ft, topk = f["E"], f["ft"], f["topk"]
                normalize(keep=L == 3, counted=True)
                nl = {0: 16, 1: 48, 2: 48, 3: 32}[L]
                gl.step(nl)
                lg.step()
                dve.wait_ge(s_lg, lg.at())
                l, pb, sl, mk, rk = (z[:, :, 0:E] for z in (LG, PB, SL, MK, RK))

                def wide(z, n=E):
                    return z[:].unsqueeze(2).to_broadcast([P, NT, n])

                def rank(z, out_, n):
                    back = WI[:, :, 0:n]

                    def later_greater(d):
                        c = BIG[d % 2][:, 0:NT, 0:n - d]
                        return c, dve.tensor_tensor(c, z[:, :, d:n], z[:, :, 0:n - d], ALU.is_gt)

                    dve.memset(out_, 0.0)
                    dve.tensor_copy(back, count_up[:, 0:n].unsqueeze(1).to_broadcast([P, NT, n]))
                    c, last = later_greater(1)
                    link(last)
                    for d in range(1, n):
                        now = c
                        if d < n - 1:
                            c, _ = later_greater(d + 1)
                        dve.tensor_tensor(out_[:, :, 0:n - d], out_[:, :, 0:n - d], now, ALU.add)
                        link(dve.tensor_tensor(back[:, :, d:n], back[:, :, d:n], now, ALU.subtract))
                    link(dve.tensor_tensor(out_, out_, back, ALU.add))

                dve.wait_ge(s_gl, gl.at())
                if L >= 2:
                    gb = GB[:, 0:E].unsqueeze(1).to_broadcast([P, NT, E])
                    link(dve.tensor_tensor(l, PS[:, 4, 0:NT * E].rearrange("p (t e) -> p t e", e=E), gb, ALU.add))
                else:
                    link(dve.tensor_copy(l, PS[:, 4, 0:NT * E].rearrange("p (t e) -> p t e", e=E)))
                if L > 0:
                    link(dve.reduce_max(R1[:], l, AX.X))
                    if L == 1:
                        rank(l, rk, E)
                    dve.tensor_tensor(l, l, wide(R1), ALU.subtract).then_inc(s_lc, 1)
                else:
                    dve.memset(R1[:], 0.0).then_inc(s_lc, 1)
                ex.step()
                dve.wait_ge(s_ex, ex.at())
                if L == 0:
                    p4 = PB[:].rearrange("p t (g i) -> p t g i", i=4)
                    s0, s1, s2, s3 = (p4[:, :, :, i] for i in range(4))
                    hi0, lo0, hi1, lo1, best, sec = (z[:] for z in T4)
                    link(dve.tensor_tensor(hi0, s0, s1, ALU.max))
                    link(dve.tensor_tensor(lo0, s0, s1, ALU.min))
                    link(dve.tensor_tensor(hi1, s2, s3, ALU.max))
                    link(dve.tensor_tensor(lo1, s2, s3, ALU.min))
                    link(dve.tensor_tensor(best, hi0, hi1, ALU.max))
                    link(dve.tensor_tensor(sec, hi0, hi1, ALU.min))
                    link(dve.tensor_tensor(lo0, lo0, lo1, ALU.max))
                    link(dve.tensor_tensor(sec, sec, lo0, ALU.max))
                    link(dve.tensor_tensor(best, best, sec, ALU.add))
                    rank(T4[4][:], T4[0][:], 4)
                    link(dve.tensor_scalar(T4[0][:], T4[0][:], 2.0, None, ALU.is_lt))
                    m4 = MK[:].rearrange("p t (g i) -> p t g i", i=4)
                    for i in range(4):
                        last = dve.tensor_tensor(m4[:, :, :, i], p4[:, :, :, i], T4[0][:], ALU.mult)
                    link(last)
                    rank(mk, rk, E)
                elif L >= 2:
                    link(dve.tensor_reduce(R1[:], pb, AX.X, ALU.add))
                    link(dve.reciprocal(R1[:], R1[:]))
                    link(dve.tensor_tensor(pb, pb, wide(R1), ALU.mult))
                    rank(pb, rk, E)
                link(dve.tensor_scalar(sl, rk, float(topk), None, ALU.is_lt))
                link(dve.tensor_tensor(pb, pb, sl, ALU.mult))
                link(dve.tensor_reduce(R1[:], pb, AX.X, ALU.add))
                if L in (0, 3):
                    link(dve.tensor_scalar(R1[:], R1[:], 1e-20 if L == 0 else 1e-9, None, ALU.add))
                link(dve.reciprocal(R1[:], R1[:]))
                if L == 0:
                    link(dve.tensor_scalar(R1[:], R1[:], 2.5, None, ALU.mult))
                cb = comb[:, :, 0:E]
                if L in (0, 2):
                    dve.tensor_tensor(cb, pb, wide(R1), ALU.mult).then_inc(s_cb, 1)
                else:
                    link(dve.tensor_tensor(pb, pb, wide(R1), ALU.mult))
                    link(dve.memset(TOT[:, 0, :], 0.0))
                    dve.sem_inc(s_cb, 1)
                    by.step()
                    dve.wait_ge(s_by, by.at())
                    for t in range(NT):
                        link(dve.tensor_tensor(TOT[:, t + 1, 0:E], TOT[:, t, 0:E], PS[:, 2, E * t:E * t + E], ALU.add))
                    pos, wi, mt = POS[:, :, 0:E], WI[:, :, 0:E], MK[:, :, 0:E]
                    link(dve.tensor_tensor(pos, TOT[:, 0:NT, 0:E],
                                           PS[:, 1, 0:NT * E].rearrange("p (t e) -> p t e", e=E), ALU.add))
                    if L == 3:
                        link(dve.tensor_scalar(wi, pos, float(CAP), None, ALU.is_lt))
                        link(dve.tensor_tensor(cb, pb, wi, ALU.mult))
                        link(dve.tensor_tensor(pos, pos, first_place[:].unsqueeze(1).to_broadcast([P, NT, E]), ALU.add))
                        link(dve.tensor_scalar(wi, wi, -1.0, -float(PLACES), ALU.add, ALU.mult))
                        link(dve.tensor_tensor(pos, pos, wi, ALU.add))
                    else:
                        link(dve.tensor_copy(cb, pb))
                        big = BIG[0][:, 0:E, 0:NT]
                        link(dve.tensor_scalar(TM[:], count_up[:], float(P), None, ALU.mult))
                        link(dve.tensor_tensor(big, TOT[:, NT, 0:E].unsqueeze(2).to_broadcast([P, E, NT]),
                                               TM[:, 0:NT].unsqueeze(1).to_broadcast([P, E, NT]), ALU.is_gt))
                        link(dve.tensor_reduce(NE[:], big, AX.X, ALU.add))
                        big = BIG[0][:, 0:E, 0:E]
                        link(dve.tensor_tensor(big, NE[:].unsqueeze(1).to_broadcast([P, E, E]), less[:, 0:E, 0:E], ALU.mult))
                        link(dve.tensor_reduce(EB[:], big, AX.X, ALU.add))
                        link(dve.tensor_tensor(EE[:], EB[:], NE[:], ALU.add))
                        link(dve.tensor_scalar(EB[:], EB[:], float(P), None, ALU.mult))
                        link(dve.tensor_tensor(pos, pos, EB[:].unsqueeze(1).to_broadcast([P, NT, E]), ALU.add))
                    for r in range(2):
                        link(dve.tensor_scalar(wi, rk, float(r), None, ALU.is_equal))
                        link(dve.tensor_tensor(mt, wi, pos, ALU.mult))
                        link(dve.tensor_reduce(IP[r][:], mt, AX.X, ALU.add))
                        link(dve.tensor_copy(IS[r][:], IP[r][:]))
                        link(dve.tensor_scalar(IP[r][:], IP[r][:], float(PLACES - 1), None, ALU.min))
                        link(dve.tensor_copy(IG[r][:], IP[r][:]))
                        link(dve.tensor_tensor(mt, wi, cb, ALU.mult))
                        link(dve.tensor_reduce(WR[r][:], mt, AX.X, ALU.add))
                    dve.sem_inc(s_cb, 1)
                    dve.sem_inc(s_ix, 1)
                    ix.step()
                if L == 1:
                    tb = TB[:]
                    link(dve.tensor_tensor(tb, count_up[:].unsqueeze(2).to_broadcast([P, TILES, 8]),
                                           EE[:].unsqueeze(1).to_broadcast([P, TILES, 8]), ALU.is_ge))
                    link(dve.tensor_reduce(TF[:], tb, AX.X, ALU.add))
                    link(dve.tensor_scalar(TF[:], TF[:], 7.0, None, ALU.min))
                    link(dve.tensor_copy(TE[:], TF[:]))
                    link(dve.memset(BT[:], 0.0))
                    for e in range(8):
                        link(dve.tensor_scalar(TM[:], TF[:], float(e), None, ALU.is_equal))
                        link(dve.tensor_tensor(tb, TM[:].unsqueeze(2).to_broadcast([P, TILES, 8]),
                                               B1[:, e, :].unsqueeze(1).to_broadcast([P, TILES, 8]), ALU.mult))
                        link(dve.tensor_tensor(BT[:], BT[:], tb, ALU.add))
                    dve.sem_inc(s_ti, 1)
                if L in (1, 2):
                    for t in range(NT):
                        by.step()
                        dve.wait_ge(s_by, by.at())
                        dve.tensor_tensor(X[:, t, :], X[:, t, :], PS[:, 4 + t % 4, 0:D], ALU.add).then_inc(s_yf, 1)
                        yf.step()

                def fetched(L):
                    buf = YG1 if L == 1 else [q[:] for q in YG]
                    for t in range(NT):
                        for r in range(2):
                            k = 2 * t + r
                            yg[k % 4].step(16)
                            dve.wait_ge(s_yg[k % 4], yg[k % 4].at())
                            if r == 1:
                                dve.wait_ge(s_ix, ix.at())
                            ix.step()
                            dve.scalar_tensor_tensor(X[:, t, :], buf[k % 4], WR[r][:, t:t + 1], X[:, t, :],
                                                     ALU.mult, ALU.add).then_inc(s_ix, 1)
                        if L == 1:
                            dve.wait_ge(s_ix, ix.at())
                            dve.bn_stats(stat[:, t, :], X[:, t, :])

                def add_tile(t, e):
                    y.step()
                    dve.wait_ge(s_y, y.at())
                    if yf.n > 3:
                        dve.wait_ge(s_yf, yf.at(3))
                    yf.step()
                    b = 4 + nyt[0] % 4
                    nyt[0] += 1
                    if isinstance(e, int):
                        c = comb[:, t, e:e + 1]
                    else:
                        c = comb[:, t, bass.ds(e, 1)]
                    dve.scalar_tensor_tensor(X[:, t, :], PS[:, b, 0:D], c, X[:, t, :], ALU.mult, ALU.add).then_inc(s_yf, 1)

                nyt = [0]
                hjob = [0]

                def expert(e):
                    for c in range(NQ + 1):
                        if c < NQ and f["gated"]:
                            for t, rows in enumerate(ft):
                                sg.step()
                                dve.wait_ge(s_sg, sg.at())
                                h.step()
                                dve.wait_ge(s_h, h.at())
                                if t == 0:
                                    if dn.n > TPQ:
                                        dve.wait_ge(s_y, dn.at(TPQ))
                                    dn.step(TPQ)
                                p = hjob[0] % 2
                                hjob[0] += 1
                                dve.tensor_tensor(HT[c % 2][0:rows, t, :], SG[p][0:rows, :],
                                                  PS[0:rows, 2 * p + 1, :], ALU.mult).then_inc(s_hr, 1)
                        if c >= 1:
                            for i in range(TPQ):
                                add_tile((c - 1) * TPQ + i, e)

                if L == 2:
                    dn.step(4 * NT)
                    with dve.Fori(0, 2) as i:
                        y.loop(i, 0, 32)
                        yf.loop(i, 0, 64)
                        for par in range(2):
                            for t in range(NT):
                                y.step()
                                dve.wait_ge(s_y, y.at())
                                for k in range(2):
                                    dve.wait_ge(s_yf, yf.at())
                                    yf.step()
                                    dve.scalar_tensor_tensor(
                                        X[:, t, :], PS[:, t % 8, k * D:(k + 1) * D],
                                        comb[:, t, bass.ds(i * 4 + par * 2 + k, 1)], X[:, t, :],
                                        ALU.mult, ALU.add).then_inc(s_yf, 1)
                        y.end(2)
                        yf.end(2)
                elif L == 1:
                    def copy_hidden():
                        for half in range(2):
                            up.step()
                            dve.wait_ge(s_up, up.at())
                            dve.tensor_copy(HA[:, half * 512:(half + 1) * 512], PS[:, half, :]).then_inc(s_uc, 1)

                    def copy_answers(par, fresh):
                        if not fresh:
                            dve.wait_ge(s_yd[par], yd[par].at())
                        yd[par].step(16)
                        y.step()
                        dve.wait_ge(s_y, y.at())
                        dve.tensor_copy(YE1[par], PS[:, 4 + par, 0:D]).then_inc(s_yc, 1)

                    def copy_rows(par):
                        tr.step()
                        dve.wait_ge(s_tr, tr.at())
                        dve.tensor_copy(XT1[par], PS[:, 6 + par, 0:D]).then_inc(s_te, 1)

                    copy_rows(0)
                    copy_rows(1)
                    copy_hidden()
                    for par in range(2):
                        copy_rows(par)
                        copy_hidden()
                        copy_answers(par, True)
                    with dve.Fori(1, TILES // 2 - 1) as i:
                        loops = [(up, 4), (y, 2), (yd[0], 16), (yd[1], 16), (tr, 2)]
                        for c, p in loops:
                            c.loop(i, 1, p)
                        for par in range(2):
                            copy_rows(par)
                            copy_hidden()
                            copy_answers(par, False)
                        for c, p in loops:
                            c.end(TILES // 2 - 2)
                    copy_rows(0)
                    for par in range(2):
                        copy_hidden()
                        copy_answers(par, False)
                    copy_answers(0, False)
                    dn.step(TILES)
                    fetched(L)
                else:
                    EA = f["EA"]
                    if L < 3:
                        with dve.Fori(0, EA // 2) as i:
                            loops = [(y, 2 * NT), (yf, 2 * NT)]
                            for c, p in loops:
                                c.loop(i, 0, p)
                            expert(i * 2)
                            expert(i * 2 + 1)
                            for c, p in loops:
                                c.end(EA // 2)
                        h.step(EA * NQ * len(ft))
                        dn.step(EA * NT)
                    else:
                        expert(16)

                        def answers(par):
                            if yd[par].n > 0:
                                dve.wait_ge(s_yd[par], yd[par].at())
                            yd[par].step(32)
                            for t in range(CT):
                                r = P if t < CT - 1 else CLAST
                                y.step()
                                dve.wait_ge(s_y, y.at())
                                dve.tensor_copy(YE[par][0:r, t, :], PS[0:r, 4 + t % 2, 0:D]).then_inc(s_yc, 1)

                        def products(par):
                            for t, rows in enumerate(ft):
                                sg.step()
                                dve.wait_ge(s_sg, sg.at())
                                h.step()
                                dve.wait_ge(s_h, h.at())
                                p = hjob[0] % 2
                                hjob[0] += 1
                                dve.tensor_tensor(HT[par][0:rows, t, 0:CAP], SG[p][0:rows, 0:CAP],
                                                  PS[0:rows, 2 * p + 1, 0:CAP], ALU.mult).then_inc(s_hr, 1)

                        products(0)
                        answers(0)
                        products(1)
                        with dve.Fori(1, 8) as i:
                            loops = [(y, 2 * CT), (sg, 2 * len(ft)), (h, 2 * len(ft)), (yd[0], 32), (yd[1], 32)]
                            for c, p in loops:
                                c.loop(i, 1, p)
                            for par in range(2):
                                answers(1 - par)
                                products(par)
                            for c, p in loops:
                                c.end(7)
                        answers(1)
                        fetched(L)
                fence(dve, fences)

        @block.tensor
        def _(pe):
            fences = [0]
            mm = pe.matmul
            xn, xtc, wa = Count(s_xn), Count(s_xtc), Count(s_wa)
            pc, vc = Count(s_pc), Count(s_vc)
            ks, ql, mr = Count(s_ks), [Count(s) for s in s_ql], Count(s_mr)
            pr, use, cs, rx, os_, ot, sf, mx = Count(s_pr), Count(s_pr), Count(s_os), Count(s_rx), Count(s_os), Count(s_ot), Count(s_sf), Count(s_mx)
            gl, cb, ctc, yf = Count(s_gl), Count(s_cb), Count(s_ctc), Count(s_yf, YF_FREE)
            w, hr = [Count(s) for s in s_w], Count(s_hr, HR_FREE)
            xe, te, yc = [Count(q) for q in s_xe], Count(s_te), Count(s_yc)
            uc, ge = Count(s_uc), Count(s_ge)
            fence(pe, fences)

            def normalize(logits=None):
                for c in range(NQ):
                    xn.step()
                    pe.wait_ge(s_xn, xn.at())
                    if xtc.n > 2:
                        pe.wait_ge(s_xtc, xtc.at(2))
                    xtc.step(2)
                    for half in range(2):
                        for i in range(TPQ):
                            last = pe.transpose(PS[:, 2 * (c % 2) + half, i * P:(i + 1) * P],
                                                XN[:, c * TPQ + i, half * P:(half + 1) * P], ident[:])
                    last.then_inc(s_xt, 1)
                    if logits and c >= 1:
                        pe.wait_ge(s_xtc, xtc.at(2))
                        logits(c - 1)
                if logits:
                    pe.wait_ge(s_xtc, xtc.at())
                    logits(NQ - 1).then_inc(s_lg, 1)
                fence(pe, fences)

            for L in range(4):
                a = ATT[L]
                dh, pw, hpg, nsub = a["dh"], a["pw"], a["hpg"], a["nsub"]
                npair, units = hpg // 2, hpg * TPQ
                normalize()

                wa.step(16 * (9 + hpg if L < 3 else 5 + hpg))
                pe.wait_ge(s_wa, wa.at())
                for u in range(16):
                    kind, m, c = 1 - u // 8, (u // 4) % 2, u % 4
                    n = Q if kind == 0 else min(Q, S - c * Q)
                    if pc.n > 3:
                        pe.wait_ge(s_pc, pc.at(3))
                    pc.step()
                    o, cols = PS[:, u % 4, 0:n], slice(m * P, (m + 1) * P)
                    if kind == 0:
                        mm(o, WQ[:, 0, cols], xnT[:, 0, c * Q:c * Q + n], start=True, stop=False)
                        mm(o, WQ[:, 1, cols], xnT[:, 1, c * Q:c * Q + n], start=False, stop=True).then_inc(s_pj, 1)
                    else:
                        mm(o, WK0[:, cols], C0[:, c * Q:c * Q + n], start=True, stop=False)
                        mm(o, WK1[:, cols], C1[:, c * Q:c * Q + n], start=False, stop=True).then_inc(s_pj, 1)
                    if u < NK:
                        if vc.n > 3:
                            pe.wait_ge(s_vc, vc.at(3))
                        vc.step()
                        r = key_rows(u)
                        o, ks_ = PS[0:r, 4 + u % 4, 0:D], slice(u * P, u * P + r)
                        mm(o, C0[:, ks_], WV0[:], start=True, stop=False)
                        mm(o, C1[:, ks_], WV1[:], start=False, stop=True).then_inc(s_vj, 1)
                fence(pe, fences)

                ks.step(16 * (12 + 4))
                pe.wait_ge(s_ks, ks.at())
                for q in range(3):
                    ql[q].step(7 * 16)
                njob, pair, used = [0], [0], [0]
                sel = sel16 if dh == 16 else sel32

                def slot_of(j):
                    return j * nsub

                def side(job):
                    bank = 5 + njob[0] % 3
                    fresh = njob[0] < 3
                    njob[0] += 1
                    if job[0] == "max":
                        _, g, u, c = job
                        if u == 0 and c == 0:
                            pe.wait_ge(s_ql[g], ql[g].at())
                    elif job[0] == "turn":
                        mx.step()
                        pe.wait_ge(s_mx, mx.at())
                    elif job[0] == "den":
                        os_.step()
                        pe.wait_ge(s_os, os_.at())
                    elif job[0] == "spread":
                        rx.step()
                        pe.wait_ge(s_rx, rx.at())
                    elif job[1] == 0:
                        if ot.n > 0:
                            pe.wait_ge(s_ot, ot.at())
                    if njob[0] == 1:
                        if sf.n > 0:
                            pe.wait_ge(s_sf, sf.at(0))
                    elif not fresh:
                        if sf.n > 2:
                            pe.wait_ge(s_sf, sf.at(2))
                    sf.step()
                    if job[0] == "max":
                        _, g, u, c = job
                        j, qt = u // TPQ, u % TPQ
                        for sub in range(nsub):
                            rows = 97 if sub == 0 else 96
                            s = slot_of(j) + sub
                            ks0 = (g * hpg + j) * nsub + sub
                            last = mm(PS[:, bank, 0:CK[c]], QS[g][0:rows, s, qt * P:(qt + 1) * P],
                                      KS[0:rows, ks0, CKO[c]:CKO[c] + CK[c]], start=sub == 0, stop=sub == nsub - 1)
                    elif job[0] == "turn":
                        last = pe.transpose(PS[0:units, bank, 0:P], MX[job[1] % 2][:, 0:units], ident[:])
                    elif job[0] == "den":
                        for i in range(TPQ):
                            last = mm(PS[:, bank, i * hpg:(i + 1) * hpg], OS[job[1] % 2][:, i * P:(i + 1) * P],
                                      sel[:, 0:hpg], start=True, stop=True)
                    elif job[0] == "spread":
                        for i in range(TPQ):
                            last = pe.transpose(PS[:, bank, i * P:(i + 1) * P], RDX[:, i * P:(i + 1) * P], ident[:])
                        ot.step()
                    else:
                        i = job[1]
                        for g in range(NG):
                            last = mm(PS[:, bank, 0:D], OT[:, g, i * P:(i + 1) * P], WO[:, g, :],
                                      start=g == 0, stop=g == NG - 1)
                    last.then_inc(s_sj, 1)

                def scores(g, k, j, i):
                    r = key_rows(k)
                    b = 2 * (pair[0] % 2)
                    if i == 0:
                        if pr.n > 1:
                            pe.wait_ge(s_pr, pr.at(1))
                        pr.step()
                    jj = 2 * j + i
                    for sub in range(nsub):
                        rows = 100 if sub == 0 else 96
                        last = mm(PS[0:r, b + i, :], KS[0:rows, (g * hpg + jj) * nsub + sub, k * P:k * P + r],
                                  QS[g][0:rows, slot_of(jj) + sub, :], start=sub == 0, stop=sub == nsub - 1)
                    if i == 1:
                        pair[0] += 1
                        last.then_inc(s_sc, 1)

                def weigh(g, k):
                    r = key_rows(k)
                    for j in range(npair):
                        use.step()
                        pe.wait_ge(s_pr, use.at())
                        for i in range(2):
                            jj = 2 * j + i
                            last = mm(PS[pw * jj:pw * jj + pw, 4, :],
                                      V[0:r, k, (g * hpg + jj) * pw:(g * hpg + jj) * pw + pw],
                                      PR[used[0] % 4][0:r, i, :], start=k == 0, stop=k == NK - 1,
                                      skip_group_check=True)
                        used[0] += 1
                        last.then_inc(s_pv, 1)

                for job in side_prologue(hpg):
                    side(job)

                def iteration(first, last):
                    njob[0] = 0
                    for g in range(NG):
                        if not (last and g > 0):
                            ql[(g + 3) % 4].step(7 * 16)
                        mr.step(16)
                        pe.wait_ge(s_mr, mr.at())
                        for k, slot in enumerate(side_schedule(g, hpg, first, last)):
                            for job in slot[:2]:
                                side(job)
                            cut = [2 + n for n in chunk_of(max(len(slot) - 2, 0), 2 * npair)]
                            for j in range(npair):
                                for i in range(2):
                                    scores(g, k, j, i)
                                    for job in slot[cut[2 * j + i]:cut[2 * j + i + 1]]:
                                        side(job)
                            if k == 0 and not (first and g == 0):
                                weigh((g - 1) % NG, NK - 1)
                            elif k > 0:
                                if k == 1 and not (first and g == 0):
                                    cs.step()
                                    pe.wait_ge(s_os, cs.at())
                                weigh(g, k - 1)

                njobs = sum(len(s) for g in range(NG) for s in side_schedule(g, hpg, False, False))
                iteration(True, False)
                with pe.Fori(1, NQ - 1) as it:
                    loops = [(mr, 64), (pr, NG * NK * npair), (use, NG * NK * npair), (cs, NG), (os_, NG), (ot, NG), (rx, NG),
                             (sf, njobs), (mx, NG)] + [(c, 7 * 16) for c in ql]
                    for c, p in loops:
                        c.loop(it, 1, p)
                    iteration(False, False)
                    for c, p in loops:
                        c.end(NQ - 2)
                iteration(False, True)
                weigh(NG - 1, NK - 1)
                njob[0] = 0
                for job in [("den", NG - 1), ("spread", NG - 1)] + [("out", i) for i in range(TPQ)]:
                    side(job)
                cs.step()
                fence(pe, fences)

                f = FFN[L]
                E, ft = f["E"], f["ft"]
                gl.step({0: 16, 1: 48, 2: 48, 3: 32}[L])
                pe.wait_ge(s_gl, gl.at())

                def logits(c):
                    for t in range(c * TPQ, (c + 1) * TPQ):
                        for k in range(2):
                            last = mm(PS[:, 4, t * E:(t + 1) * E], xnT[:, k, t * P:(t + 1) * P], GW[:, k, 0:E],
                                      start=k == 0, stop=k == 1)
                    return last

                normalize(logits)
                cb.step()
                pe.wait_ge(s_cb, cb.at())
                if L in (1, 3):
                    sl, n = SL[:, :, 0:E], NT * E
                    mm(PS[:, 1, 0:n].rearrange("p (t e) -> p t e", e=E), tri[:], sl, start=True, stop=True)
                    mm(PS[:, 2, 0:n].rearrange("p (t e) -> p t e", e=E), ones[:], sl, start=True, stop=True)\
                        .then_inc(s_by, 1)
                    cb.step()
                    pe.wait_ge(s_cb, cb.at())
                if L in (1, 2):
                    for c in range(NQ):
                        if ctc.n > 1:
                            pe.wait_ge(s_ctc, ctc.at(1))
                        ctc.step()
                        for i in range(TPQ):
                            last = pe.transpose(PS[0:8, c % 2, i * P:(i + 1) * P], comb[:, c * TPQ + i, 0:8], ident[:])
                        last.then_inc(s_ct, 1)
                    pe.wait_ge(s_ctc, ctc.at())
                    for t in range(NT):
                        if yf.n > 3:
                            pe.wait_ge(s_yf, yf.at(3))
                        yf.step()
                        mm(PS[:, 4 + t % 4, 0:D], combT[:, t * P:(t + 1) * P], B2[:], start=True, stop=True).then_inc(s_by, 1)

                hj, yj = [0], [0]

                def expert(par):
                    F = sum(ft)
                    W = 2 * F if f["gated"] else F
                    w[par].step({0: 32, 3: 48}[L])
                    pe.wait_ge(s_w[par], w[par].at())
                    up = WU[par][:, 0:2 * W].rearrange("p (k f) -> p k f", k=2)
                    for c in range(NQ + 1):
                        if c < NQ:
                            at = 0
                            for t, rows in enumerate(ft):
                                if f["gated"]:
                                    if hr.n > 1:
                                        pe.wait_ge(s_hr, hr.at(1))
                                    banks = [(2 * (hj[0] % 2), 0), (2 * (hj[0] % 2) + 1, F)]
                                else:
                                    if hr.n > 3:
                                        pe.wait_ge(s_hr, hr.at(3))
                                    banks = [(hj[0] % 4, 0)]
                                hr.step()
                                hj[0] += 1
                                for b, off in banks:
                                    for k in range(2):
                                        last = mm(PS[0:rows, b, :], up[:, k, off + at:off + at + rows],
                                                  xnT[:, k, c * Q:(c + 1) * Q], start=k == 0, stop=k == 1)
                                at += rows
                                last.then_inc(s_h, 1)
                        if c >= 1:
                            lag = len(ft) if c < NQ else 0
                            if hr.n > lag:
                                pe.wait_ge(s_hr, hr.at(lag))
                            for i in range(TPQ):
                                if yf.n > 3:
                                    pe.wait_ge(s_yf, yf.at(3))
                                yf.step()
                                b = 4 + yj[0] % 4
                                yj[0] += 1
                                for t, rows in enumerate(ft):
                                    last = mm(PS[:, b, 0:D], HT[(c - 1) % 2][0:rows, t, i * P:(i + 1) * P],
                                              WD[par][0:rows, t, :], start=t == 0, stop=t == len(ft) - 1)
                                last.then_inc(s_y, 1)

                if L == 2:
                    pe.wait_ge(s_yf, yf.at())
                    with pe.Fori(0, 2) as i:
                        loops = [(yf, 64), (w[0], 16), (w[1], 16)]
                        for c, p in loops:
                            c.loop(i, 0, p)
                        for par in range(2):
                            w[par].step(16)
                            pe.wait_ge(s_w[par], w[par].at())
                            for t in range(NT):
                                if yf.n > 14:
                                    pe.wait_ge(s_yf, yf.at(14))
                                yf.step(2)
                                for k in range(2):
                                    last = mm(PS[:, t % 8, :], xnT[:, k, t * P:(t + 1) * P],
                                              WU[par][:, k * 512:(k + 1) * 512], start=k == 0, stop=k == 1)
                                last.then_inc(s_y, 1)
                        for c, p in loops:
                            c.end(2)
                elif L == 1:
                    def rows_in(par):
                        xe[par].step(16)
                        pe.wait_ge(s_xe[par], xe[par].at())
                        te.step()
                        for half in range(2):
                            last = pe.transpose(PS[:, 6 + par, half * P:(half + 1) * P],
                                                XE1[par][:, half * P:(half + 1) * P], ident[:])
                        last.then_inc(s_tr, 1)

                    def project(e, par, ahead=1):
                        pe.wait_ge(s_te, te.at(ahead))
                        pe.wait_ge(s_wr, e + 1)
                        if uc.n > 0:
                            pe.wait_ge(s_uc, uc.at())
                        uc.step(2)
                        for half in range(2):
                            for k in range(2):
                                w1 = WA[:, bass.ds(e, 1), k * NF + half * 512:k * NF + (half + 1) * 512]
                                last = mm(PS[:, half, :], XT1[par][:, k * P:(k + 1) * P],
                                          w1.rearrange("p a f -> p (a f)"), start=k == 0, stop=k == 1)
                            last.then_inc(s_up, 1)

                    def turn_hidden():
                        if ge.n > 0:
                            pe.wait_ge(s_ge, ge.at())
                        ge.step()
                        pe.wait_ge(s_uc, uc.at(1))
                        for q in range(NF // P):
                            if q == NF // P // 2:
                                pe.wait_ge(s_uc, uc.at())
                            last = pe.transpose(PS[:, 2 + q // 4, q % 4 * P:(q % 4 + 1) * P],
                                                HA[:, q * P:(q + 1) * P], ident[:])
                        last.then_inc(s_ut, 1)

                    def answer(e, par):
                        pe.wait_ge(s_ge, ge.at())
                        for q in range(NF // P):
                            w2 = WA[:, bass.ds(e, 1), 2 * NF + q * D:2 * NF + (q + 1) * D]
                            last = mm(PS[:, 4 + par, 0:D], HB[:, q * P:(q + 1) * P],
                                      w2.rearrange("p a f -> p (a f)"), start=q == 0, stop=q == NF // P - 1)
                        last.then_inc(s_y, 1)

                    def expert_of(i):
                        return pe.value_load(TE[0:1, bass.ds(i, 1)], min_val=0, max_val=7)

                    pe.wait_ge(s_yf, yf.at())
                    pe.wait_ge(s_ti, 1)
                    rows_in(0)
                    rows_in(1)
                    project(expert_of(0), 0)
                    turn_hidden()
                    with pe.Fori(1, TILES // 2) as i:
                        loops = [(xe[0], 16), (xe[1], 16), (te, 2), (uc, 4), (ge, 2)]
                        for c, p in loops:
                            c.loop(i, 1, p)
                        for par in range(2):
                            before, now = expert_of(i * 2 - 2 + par), expert_of(i * 2 - 1 + par)
                            rows_in(par)
                            project(now, 1 - par)
                            answer(before, par)
                            turn_hidden()
                        for c, p in loops:
                            c.end(TILES // 2 - 1)
                    for j in range(TILES - 2, TILES):
                        before, now = expert_of(j - 1), expert_of(j)
                        if j == TILES - 2:
                            rows_in(0)
                        project(now, j % 2, TILES - 1 - j)
                        answer(before, (j - 1) % 2)
                        turn_hidden()
                    answer(expert_of(TILES - 1), 0)
                    yc.step(TILES)
                else:
                    EA = f["EA"]
                    nw = {0: 32, 3: 48}[L]
                    if L < 3:
                        with pe.Fori(0, EA // 2) as i:
                            loops = [(hr, 2 * NQ * len(ft)), (yf, 2 * NT), (w[0], nw), (w[1], nw)]
                            for c, p in loops:
                                c.loop(i, 0, p)
                            expert(0)
                            expert(1)
                            for c, p in loops:
                                c.end(EA // 2)
                    else:
                        expert(0)
                        pe.wait_ge(s_yf, yf.at())

                        def rows_in(par):
                            xe[par].step(32)
                            pe.wait_ge(s_xe[par], xe[par].at())
                            if te.n > 0:
                                pe.wait_ge(s_te, te.at())
                            te.step()
                            for half in range(2):
                                for t in range(CT):
                                    r = P if t < CT - 1 else CLAST
                                    last = pe.transpose(PS[:, 6 + half, t * P:t * P + r],
                                                        XE[par][0:r, t, half * P:(half + 1) * P], ident[0:r, 0:r])
                            last.then_inc(s_tr, 1)

                        def hidden(par):
                            F = sum(ft)
                            w[1 - par].step(nw)
                            pe.wait_ge(s_w[1 - par], w[1 - par].at())
                            pe.wait_ge(s_te, te.at())
                            up = WU[1 - par][:, 0:4 * F].rearrange("p (k f) -> p k f", k=2)
                            at = 0
                            for t, rows in enumerate(ft):
                                pe.wait_ge(s_hr, hr.at(1))
                                hr.step()
                                b = 2 * (hj[0] % 2)
                                hj[0] += 1
                                for v in range(2):
                                    for k in range(2):
                                        last = mm(PS[0:rows, b + v, 0:CAP], up[:, k, v * F + at:v * F + at + rows],
                                                  XT[par][:, k, :], start=k == 0, stop=k == 1)
                                at += rows
                                last.then_inc(s_h, 1)

                        def answer(par):
                            pe.wait_ge(s_hr, hr.at())
                            for t in range(CT):
                                r = P if t < CT - 1 else CLAST
                                if yc.n > 1:
                                    pe.wait_ge(s_yc, yc.at(1 if t else 0))
                                yc.step()
                                for q, rows in enumerate(ft):
                                    last = mm(PS[0:r, 4 + t % 2, 0:D], HT[par][0:rows, q, t * P:t * P + r],
                                              WD[1 - par][0:rows, q, :], start=q == 0, stop=q == len(ft) - 1)
                                last.then_inc(s_y, 1)

                        rows_in(0)
                        hidden(0)
                        rows_in(1)
                        answer(0)
                        hidden(1)
                        with pe.Fori(1, 8) as i:
                            loops = [(hr, 2 * len(ft)), (w[0], nw), (w[1], nw), (xe[0], 32), (xe[1], 32),
                                     (te, 2), (yc, 2 * CT)]
                            for c, p in loops:
                                c.loop(i, 1, p)
                            for par in range(2):
                                rows_in(par)
                                answer(1 - par)
                                hidden(par)
                            for c, p in loops:
                                c.end(7)
                        answer(1)
                fence(pe, fences)


def kernel(x, ctx_768, mask_BxS2_bf1, **w):
    import numpy as np
    import concourse.bacc as bacc
    from concourse.bass_utils import run_bass_kernel_spmd

    w = {k: np.asarray(v) for k, v in w.items()}
    a = {}

    def contraction_first(m, n):
        lead = m.shape[:-2]
        m = m.reshape(*lead, n, P, m.shape[-1])
        return np.moveaxis(m, -3, -2).reshape(*lead, P, n * m.shape[-1])

    a["x"] = np.asarray(x)[0]
    a["ctx_t"] = np.asarray(ctx_768)[0].T
    a["mask"] = np.asarray(mask_BxS2_bf1).view(np.uint8)
    wkv = w["L0_xattn_Wkv"].reshape(16, 2, 16, DC)
    bkv = w["L0_xattn_bkv"].reshape(16, 2, 16)
    a["wq0"], a["bq0"] = w["L0_xattn_Wq"].T, w["L0_xattn_bq"]
    a["wk0"], a["bk0"] = wkv[:, 0].reshape(D, DC).T, bkv[:, 0].reshape(D)
    a["wv0"], a["bv0"] = wkv[:, 1].reshape(D, DC).T, bkv[:, 1].reshape(D)
    a["wo0"], a["bo0"] = w["L0_xattn_Wo"].T, w["L0_xattn_bo"]
    for n in "qkvo":
        a[f"w{n}1"], a[f"b{n}1"] = w[f"L1_xattn_w{n}"], w[f"L1_xattn_b{n}"]
        a[f"w{n}2"], a[f"b{n}2"] = w[f"L2_xattn_W{n}"].T, w[f"L2_xattn_b{n}"]
        a[f"w{n}3"] = w[f"L3_xattn_W{n}"]
    a["gw0"], a["gw1"] = w["L0_ffn_gate_weight"].T, w["L1_ffn_router_w"].T
    a["gw2"], a["gb2"] = w["L2_ffn_Wg"], w["L2_ffn_bg"]
    a["gw3"], a["gb3"] = w["L3_ffn_router_w"], w["L3_ffn_router_b"]
    up = np.concatenate([w["L0_ffn_expert_up"], np.moveaxis(w["L0_ffn_shared_up"].reshape(D, 4, P), 1, 0)])
    a["up0"] = contraction_first(up, 2)
    a["down0"] = np.concatenate([w["L0_ffn_expert_down"], w["L0_ffn_shared_down"].reshape(4, P, D)])
    a["up1"] = contraction_first(np.swapaxes(w["L1_ffn_w1"], 1, 2), 2)
    a["down1"] = contraction_first(np.swapaxes(w["L1_ffn_w2"], 1, 2), 8)
    a["b1"] = np.swapaxes(w["L1_ffn_b1"].reshape(8, 8, P), 1, 2)
    a["b2_1"], a["b2_2"] = w["L1_ffn_b2"], w["L2_ffn_be"]
    we = np.moveaxis(w["L2_ffn_We"].reshape(4, 2, D, D), 3, 1).reshape(4, D, 2 * D)
    a["we2"] = contraction_first(we, 2)
    gate = np.concatenate([w["L3_ffn_w_gate"], w["L3_ffn_sw_gate"][None]])
    upw = np.concatenate([w["L3_ffn_w_up"], w["L3_ffn_sw_up"][None]])
    down = np.concatenate([w["L3_ffn_w_down"], w["L3_ffn_sw_down"][None]])
    a["up3"] = contraction_first(np.concatenate([gate, upw], axis=-1), 2)
    a["down3"] = contraction_first(down[:, 0:2 * P], 2)
    a["down3b"] = down[:, 2 * P:]

    nc = bacc.Bacc("TRN2", target_bir_lowering=False, num_devices=1)
    arrays, aps = {}, {}
    for name, v in a.items():
        v = np.ascontiguousarray(v)
        arrays[f"in_{name}"] = v
        aps[name] = nc.dram_tensor(f"in_{name}", v.shape, mybir.dt.from_np(v.dtype), kind="ExternalInput").ap()
    out = nc.dram_tensor("out_x", (T, D), mybir.dt.float32, kind="ExternalOutput").ap()
    build(nc, aps, out)
    r = run_bass_kernel_spmd(nc, [arrays], core_ids=[0])
    return r.results[0]["out_x"].reshape(1, T, D)
```
